# Optimizing a Trainium2 kernel written in Bass

```python
import numpy as np
import jax
import jax.numpy as jnp

def _softmax(x, axis=-1):
    return jax.nn.softmax(x, axis=axis)

def _gelu(x):
    return jax.nn.gelu(x, approximate=True)

def _silu(x):
    return jax.nn.silu(x)

def _sigmoid(x):
    return jax.nn.sigmoid(x)

def _layernorm(x, axis=-1, eps=1e-05):
    m = jnp.mean(x, axis=axis, keepdims=True)
    v = jnp.var(x, axis=axis, keepdims=True)
    return (x - m) / jnp.sqrt(v + eps)

def _scatter_add(tgt, idx, src, axis=0):
    return tgt.at[idx].add(src)

def _segment_sum(src, seg, n):
    return jax.ops.segment_sum(src, seg, n)
kernel_name = 'mk_audio_tower_d1_tok_audfeat512_r4_c2ee38'

def setup_inputs(seed: int=0):
    np.random.seed(seed)
    _w = jnp.asarray

    def _rec_inputs():
        import jax
        import jax.numpy as jnp
        _rk = jax.random.key(seed)
        x = 3.78913e-05 + 1.00016 * jax.random.normal(jax.random.fold_in(_rk, 1), (32, 500, 64), jnp.float32)
        return x
    x = _rec_inputs()

    def _L0_tok_setup():
        import jax, jax.numpy as jnp
        import numpy as np
        CONTEXT = 5
        DILATION = 1
        EPS = 1e-05
        key = jax.random.key(seed)
        k1, k2, k3 = jax.random.split(key, 3)
        B, T, D, O = (64, 500, 64, 128)
        x = jax.random.normal(k1, (B, T, D), dtype=jnp.float32)
        K = D * CONTEXT
        W = jax.random.normal(k2, (O, K), dtype=jnp.float32) / np.sqrt(K).astype(np.float32)
        b = jax.random.normal(k3, (O,), dtype=jnp.float32) * 0.01
        gamma = jnp.ones((O,), dtype=jnp.float32)
        beta = jnp.zeros((O,), dtype=jnp.float32)
        return {'x': x, 'W': W, 'b': b, 'gamma': gamma, 'beta': beta}
    _L0_tok_all = _L0_tok_setup()
    _L0_tok_in = {k: v for k, v in _L0_tok_all.items() if k in ('W', 'b', 'gamma', 'beta')}
    del _L0_tok_all

    def _L0_attn_setup():
        import jax, jax.numpy as jnp
        import numpy as np
        EMBED_DIM = 128
        N_HEADS = 8
        HEAD_DIM = EMBED_DIM // N_HEADS
        B, S = (4, 512)

        def gelu(x):
            return jax.nn.gelu(x, approximate=False)
        key = jax.random.key(seed)
        ks = jax.random.split(key, 9)
        sc = 1.0 / np.sqrt(EMBED_DIM)
        inp = {'x': jax.random.normal(ks[0], (B, S, EMBED_DIM), dtype=jnp.float32), 'Wq': jax.random.uniform(ks[1], (EMBED_DIM, EMBED_DIM), jnp.float32, -sc, sc), 'bq': jax.random.uniform(ks[2], (EMBED_DIM,), jnp.float32, -sc, sc), 'Wk': jax.random.uniform(ks[3], (EMBED_DIM, EMBED_DIM), jnp.float32, -sc, sc), 'bk': jax.random.uniform(ks[4], (EMBED_DIM,), jnp.float32, -sc, sc), 'Wv': jax.random.uniform(ks[5], (EMBED_DIM, EMBED_DIM), jnp.float32, -sc, sc), 'bv': jax.random.uniform(ks[6], (EMBED_DIM,), jnp.float32, -sc, sc), 'Wo': jax.random.uniform(ks[7], (EMBED_DIM, EMBED_DIM), jnp.float32, -sc, sc), 'bo': jax.random.uniform(ks[8], (EMBED_DIM,), jnp.float32, -sc, sc)}
        return inp
    _L0_attn_all = _L0_attn_setup()
    _L0_attn_in = {k: v for k, v in _L0_attn_all.items() if k in ('Wq', 'bq', 'Wk', 'bk', 'Wv', 'bv', 'Wo', 'bo')}
    del _L0_attn_all

    def _L0_ffn_setup():
        import jax, jax.numpy as jnp
        import numpy as np
        B, T, I, H, S = (64, 128, 128, 128, 4)

        def _lstm_activate(gates, c):
            i, f, g, o = jnp.split(gates, 4, axis=-1)
            c_new = jax.nn.sigmoid(f) * c + jax.nn.sigmoid(i) * jnp.tanh(g)
            h_new = jax.nn.sigmoid(o) * jnp.tanh(c_new)
            return (h_new, c_new)
        key = jax.random.key(seed)
        ks = jax.random.split(key, 7)
        sc_i = 1.0 / np.sqrt(I)
        sc_h = 1.0 / np.sqrt(H)
        x = jax.random.normal(ks[0], (B, T, I), jnp.float32)
        W_ih = jax.random.normal(ks[1], (S, 4 * H, I), jnp.float32) * sc_i
        W_hh = jax.random.normal(ks[2], (S, 4 * H, H), jnp.float32) * sc_h
        b_ih = jax.random.normal(ks[3], (S, 4 * H), jnp.float32) * sc_h
        b_hh = jax.random.normal(ks[4], (S, 4 * H), jnp.float32) * sc_h
        W_sel = jax.random.normal(ks[5], (S, 2 * H + I), jnp.float32) * sc_h
        b_sel = jax.random.normal(ks[6], (S,), jnp.float32) * sc_h
        return {'x': x, 'W_ih': W_ih, 'W_hh': W_hh, 'b_ih': b_ih, 'b_hh': b_hh, 'W_sel': W_sel, 'b_sel': b_sel}
    _L0_ffn_all = _L0_ffn_setup()
    _L0_ffn_in = {k: v for k, v in _L0_ffn_all.items() if k in ('W_ih', 'W_hh', 'b_ih', 'b_hh', 'W_sel', 'b_sel')}
    del _L0_ffn_all
    return {'x': x, 'L0_tok_W': _L0_tok_in['W'], 'L0_tok_b': _L0_tok_in['b'], 'L0_tok_gamma': _L0_tok_in['gamma'], 'L0_tok_beta': _L0_tok_in['beta'], 'L0_attn_Wq': _L0_attn_in['Wq'], 'L0_attn_bq': _L0_attn_in['bq'], 'L0_attn_Wk': _L0_attn_in['Wk'], 'L0_attn_bk': _L0_attn_in['bk'], 'L0_attn_Wv': _L0_attn_in['Wv'], 'L0_attn_bv': _L0_attn_in['bv'], 'L0_attn_Wo': _L0_attn_in['Wo'], 'L0_attn_bo': _L0_attn_in['bo'], 'L0_ffn_W_ih': _L0_ffn_in['W_ih'], 'L0_ffn_W_hh': _L0_ffn_in['W_hh'], 'L0_ffn_b_ih': _L0_ffn_in['b_ih'], 'L0_ffn_b_hh': _L0_ffn_in['b_hh'], 'L0_ffn_W_sel': _L0_ffn_in['W_sel'], 'L0_ffn_b_sel': _L0_ffn_in['b_sel']}

def reference(x, L0_tok_W, L0_tok_b, L0_tok_gamma, L0_tok_beta, L0_attn_Wq, L0_attn_bq, L0_attn_Wk, L0_attn_bk, L0_attn_Wv, L0_attn_bv, L0_attn_Wo, L0_attn_bo, L0_ffn_W_ih, L0_ffn_W_hh, L0_ffn_b_ih, L0_ffn_b_hh, L0_ffn_W_sel, L0_ffn_b_sel):
    import jax
    import jax.numpy as jnp

    def _L0_tok_ref(x, W, b, gamma, beta):
        import jax, jax.numpy as jnp
        import numpy as np
        CONTEXT = 5
        DILATION = 1
        EPS = 1e-05
        B, T, D = x.shape
        new_T = T - DILATION * (CONTEXT - 1)
        win = jnp.concatenate([x[:, i * DILATION:i * DILATION + new_T, :] for i in range(CONTEXT)], axis=-1)
        y = jnp.einsum('btk,ok->bto', win, W) + b
        y = jax.nn.relu(y)
        mean = jnp.mean(y, axis=(0, 1))
        var = jnp.mean(jnp.square(y - mean), axis=(0, 1))
        y = (y - mean) * jax.lax.rsqrt(var + EPS) * gamma + beta
        return y

    def _L0_attn_ref(x, Wq, bq, Wk, bk, Wv, bv, Wo, bo):
        import jax, jax.numpy as jnp
        import numpy as np
        EMBED_DIM = 128
        N_HEADS = 8
        HEAD_DIM = EMBED_DIM // N_HEADS
        B, S = (4, 512)

        def gelu(x):
            return jax.nn.gelu(x, approximate=False)
        Bsz, Ssz, _ = x.shape

        def proj(W, b):
            h = gelu(jnp.einsum('bse,ef->bsf', x, W.T) + b)
            return h.reshape(Bsz, Ssz, N_HEADS, HEAD_DIM).transpose(0, 2, 1, 3)
        q = proj(Wq, bq)
        k = proj(Wk, bk)
        v = proj(Wv, bv)
        attn = jnp.einsum('bhid,bhjd->bhij', q, k) / np.sqrt(HEAD_DIM).astype(np.float32)
        attn = jax.nn.softmax(attn, axis=-1)
        o = jnp.einsum('bhij,bhjd->bhid', attn, v)
        o = o.transpose(0, 2, 1, 3).reshape(Bsz, Ssz, EMBED_DIM)
        return gelu(jnp.einsum('bse,ef->bsf', o, Wo.T) + bo)

    def _L0_ffn_ref(x, W_ih, W_hh, b_ih, b_hh, W_sel, b_sel):
        import jax, jax.numpy as jnp
        import numpy as np
        B, T, I, H, S = (64, 128, 128, 128, 4)

        def _lstm_activate(gates, c):
            i, f, g, o = jnp.split(gates, 4, axis=-1)
            c_new = jax.nn.sigmoid(f) * c + jax.nn.sigmoid(i) * jnp.tanh(g)
            h_new = jax.nn.sigmoid(o) * jnp.tanh(c_new)
            return (h_new, c_new)
        Bx, Tx, Ix = x.shape
        Sx, fourH, _ = W_ih.shape
        Hx = fourH // 4
        c0 = jnp.zeros((Bx, Hx), x.dtype)
        g0 = x[:, 0] @ W_ih[0].T + b_ih[0] + b_hh[0]
        h, c = _lstm_activate(g0, c0)

        def step(carry, x_t):
            h, c = carry
            sel_in = jnp.concatenate([h, c, x_t], axis=-1)
            logits = sel_in @ W_sel.T + b_sel
            onehot = jax.nn.one_hot(jnp.argmax(logits, axis=-1), Sx, dtype=x_t.dtype)
            g_all = jnp.einsum('bi,sgi->bsg', x_t, W_ih) + jnp.einsum('bh,sgh->bsg', h, W_hh) + b_ih + b_hh
            g = jnp.einsum('bsg,bs->bg', g_all, onehot)
            h2, c2 = _lstm_activate(g, c)
            return ((h2, c2), h2)
        xs = jnp.swapaxes(x[:, 1:], 0, 1)
        (_, _), hs = jax.lax.scan(step, (h, c), xs)
        outputs = jnp.concatenate([h[:, None], jnp.swapaxes(hs, 0, 1)], axis=1)
        return outputs
    h = _L0_tok_ref(x, L0_tok_W, L0_tok_b, L0_tok_gamma, L0_tok_beta)
    h = h + _L0_attn_ref(_layernorm(h, axis=-1), L0_attn_Wq, L0_attn_bq, L0_attn_Wk, L0_attn_bk, L0_attn_Wv, L0_attn_bv, L0_attn_Wo, L0_attn_bo)
    h = h + _L0_ffn_ref(_layernorm(h, axis=-1), L0_ffn_W_ih, L0_ffn_W_hh, L0_ffn_b_ih, L0_ffn_b_hh, L0_ffn_W_sel, L0_ffn_b_sel)
    return h

_drawn_inputs = setup_inputs


def setup_inputs(seed=0):
    import zlib

    import numpy as np

    out = dict(_drawn_inputs(seed))
    spreads = {'L0_tok_gamma': (1.0, 0.2), 'L0_tok_beta': (0.0, 0.1)}
    factors = {'L0_attn_Wq': 7.19, 'L0_attn_bq': 8.0, 'L0_attn_Wk': 6.468, 'L0_attn_bk': 8.0}
    for name, (base, spread) in spreads.items():
        noise = np.random.default_rng([zlib.crc32(name.encode()), seed]).standard_normal(out[name].shape)
        drawn = base * np.exp(spread * noise) if base else spread * noise
        out[name] = jnp.asarray(drawn.astype(out[name].dtype))
    for name, factor in factors.items():
        out[name] = (out[name] * factor).astype(out[name].dtype)
    return out
```

```python
import concourse.bass as bass
from concourse import mybir
from contextlib import ExitStack

B, T_IN, D, TAPS = 32, 500, 64, 5
T = T_IN - TAPS + 1
C = 128
HEADS, HD = 8, 16
CH = 124
NCH = T // CH
S = 4
EPS = 1e-5
STEPS = 16
PIECES = 4

K_ID, K_PICK, K_CENTRE, K_MEAN, K_FIRST, K_PAR, K_IND, K_PART, K_SEL0 = range(9)
WIDTHS = [C, C, C, C, S, 2, C, 3, C]
COLS = [sum(WIDTHS[:n]) for n in range(len(WIDTHS) + 1)]


def audio_tower(nc, x, tok_w, tok_v, attn_w, attn_b, w_ih, w_hh, w_sel, b_ih, b_hh, b_sel, consts, vmask, out):
    f32, bf16 = mybir.dt.float32, mybir.dt.bfloat16
    ALU, ACT = mybir.AluOpType, mybir.ActivationFunctionType
    AX = mybir.AxisListType.X

    def at_least(eng, sem, n):
        if not (isinstance(n, int) and n <= 0):
            eng.wait_ge(sem, n)

    def rounds(eng, body, total, tail=0):
        body(0, 0)
        body(1, 1)
        with eng.Fori(1, total // 2) as i:
            body(2 * i, 0)
            body(2 * i + 1, 1)
        for n in range(total, total + tail):
            body(n, n % 2)

    stack = ExitStack()
    with stack:
        def sb(name, shape, dt=f32, on=stack):
            return on.enter_context(nc.sbuf_tensor(name, shape, dt))

        def ps(name, on=stack):
            return on.enter_context(nc.psum_tensor(name, [128, 512], f32))

        def sem(name):
            return stack.enter_context(nc.semaphore(name))

        Y = sb("Y", [C, B, T])
        X = sb("X", [C, B * T_IN])
        XH = X[:, 0:B * T].rearrange("p (b t) -> p b t", b=B)
        kc = sb("kc", [128, COLS[-1]])

        def const(k):
            return kc[:, COLS[k]:COLS[k] + WIDTHS[k]]

        ident, pick, centre, mean_m, first_w, par_m = (const(k) for k in range(6))
        tokw = sb("tokw", [128, 3, C])
        tokv = sb("tokv", [C, 3])
        bn = sb("bn", [C, 4])
        eps = sb("eps", [128, 1])
        aw = sb("aw", [C, 4, C])
        ab = sb("ab", [C, 4])
        q_d = nc.dram_tensor("q_scratch", [B, C, T], f32, kind="Internal").ap()
        k_d = nc.dram_tensor("k_scratch", [B, C, T], f32, kind="Internal").ap()
        v_d = nc.dram_tensor("v_scratch", [B, CH, NCH * C], f32, kind="Internal").ap()

        with ExitStack() as p:
            stats = sb("stats", [C, B, 6], on=p)
            mv = sb("mv", [C, 2], on=p)
            cps = [ps(f"conv{i}", on=p) for i in range(2)]
            s_par, s_eps = sem("params_loaded"), sem("eps_set")
            s_x = [sem(f"x_loaded{i}") for i in range(PIECES)]
            s_conv, s_relu, s_st = sem("conv_ready"), sem("relu_ready"), sem("stats_ready")
            s_mv, s_std, s_bn = sem("bn_moments"), sem("bn_std"), sem("bn_chain")
            block = p.enter_context(nc.Block())
            half = B * T_IN // PIECES

            @block.sync
            def _(sp):
                sp.dma_start(tokw[:, :, :], tok_w).then_inc(s_par, 16)
                sp.dma_start(tokv[:, :], tok_v).then_inc(s_par, 16)
                for i in range(PIECES):
                    n = min(half, B * T_IN - 1 - i * half)
                    sp.dma_start(X[0:D, i * half:(i + 1) * half], x[:, i * half:(i + 1) * half]).then_inc(s_x[i], 16)
                    sp.dma_start(X[D:2 * D, i * half:i * half + n], x[:, i * half + 1:i * half + 1 + n]).then_inc(s_x[i], 16)
                sp.dma_start(kc[:, :], consts).then_inc(s_par, 16)
                sp.dma_start(aw[:, :, :], attn_w).then_inc(s_par, 16)
                sp.dma_start(ab[:, :], attn_b).then_inc(s_par, 16)
                sp.wait_ge(s_par, 80)

            @block.tensor
            def _(pe):
                pe.wait_ge(s_par, 80)

                def seq(n, par):
                    at_least(pe, s_relu, n - 1)
                    at = n * T_IN
                    nc.tensor.matmul(cps[par][:, 0:T], tokw[:, 0, :], X[:, bass.ds(at, T)], start=True, stop=False)
                    nc.tensor.matmul(cps[par][:, 0:T], tokw[:, 1, :], X[:, bass.ds(at + 2, T)], start=False, stop=False)
                    nc.tensor.matmul(cps[par][:, 0:T], tokw[0:D, 2, :], X[0:D, bass.ds(at + 4, T)],
                                     start=False, stop=True).then_inc(s_conv, 1)

                each = B // PIECES
                for i in range(PIECES):
                    pe.wait_ge(s_x[i], 32)
                    if i + 1 < PIECES:
                        pe.wait_ge(s_x[i + 1], 32)
                    if i == 0:
                        seq(0, 0)
                        seq(1, 1)
                    with pe.Fori(i * each // 2 + (1 if i == 0 else 0), (i + 1) * each // 2) as n:
                        seq(2 * n, 0)
                        seq(2 * n + 1, 1)

            @block.scalar
            def _(act):
                act.wait_ge(s_par, 80)

                def seq(n, par):
                    act.wait_ge(s_conv, n + 1)
                    nc.scalar.activation(Y[:, n, :], cps[par][:, 0:T], ACT.Relu, bias=tokv[:, 0:1]).then_inc(s_relu, 1)

                rounds(act, seq, B)
                act.wait_ge(s_mv, 1)
                act.wait_ge(s_eps, 1)
                nc.scalar.activation(bn[:, 0:1], mv[:, 1:2], ACT.Sqrt, bias=eps[:, 0:1]).then_inc(s_std, 1)

            @block.vector
            def _(dve):
                nc.vector.memset(eps[:, :], EPS).then_inc(s_eps, 1)

                def seq(n, par):
                    dve.wait_ge(s_relu, n + 1)
                    nc.vector.bn_stats(stats[:, n, :], Y[:, n, :]).then_inc(s_st, 1)

                rounds(dve, seq, B)
                dve.wait_ge(s_st, B)
                nc.vector.bn_aggr(mv[:, :], stats[:, :, :].rearrange("p b s -> p (b s)")).then_inc(s_mv, 1)
                dve.wait_ge(s_std, 1)
                nc.vector.reciprocal(bn[:, 1:2], bn[:, 0:1]).then_inc(s_bn, 1)
                dve.wait_ge(s_bn, 1)
                nc.vector.tensor_tensor(bn[:, 2:3], bn[:, 1:2], tokv[:, 1:2], ALU.mult).then_inc(s_bn, 1)
                dve.wait_ge(s_bn, 2)
                nc.vector.tensor_tensor(bn[:, 3:4], mv[:, 0:1], bn[:, 2:3], ALU.mult).then_inc(s_bn, 1)
                dve.wait_ge(s_bn, 3)
                nc.vector.tensor_tensor(bn[:, 3:4], tokv[:, 2:3], bn[:, 3:4], ALU.subtract).then_inc(s_bn, 1)

        def layer_norm(tag, batch_norm):
            with ExitStack() as p:
                sq = [sb(f"{tag}sq{i}", [C, T], on=p) for i in range(2)]
                rb = [sb(f"{tag}rb{i}", [C, T], on=p) for i in range(2)]
                sd = [sb(f"{tag}sd{i}", [CH, 2 * NCH], on=p) for i in range(2)]
                cen = [ps(f"{tag}cen{i}", on=p) for i in range(2)]
                var = [ps(f"{tag}var{i}", on=p) for i in range(2)]
                spr = [ps(f"{tag}spr{i}", on=p) for i in range(2)]
                s_h, s_cen, s_sq, s_var = (sem(tag + n) for n in ("h_ready", "centred", "squared", "var_ready"))
                s_sd, s_rs, s_spr, s_rb, s_xh = (sem(tag + n) for n in ("std_ready", "rstd_ready", "spread", "rstd_in_sbuf", "xhat_ready"))
                block = p.enter_context(nc.Block())

                @block.tensor
                def _(pe):
                    def seq(n, par):
                        o = 1 - par
                        if not (isinstance(n, int) and n >= B):
                            if batch_norm:
                                pe.wait_ge(s_h, n + 1)
                            at_least(pe, s_xh, n - 1)
                            nc.tensor.matmul(cen[par][:, 0:T], centre, Y[:, n, :], start=True, stop=True).then_inc(s_cen, 1)
                        if not (isinstance(n, int) and n == 0):
                            pe.wait_ge(s_rs, n)
                            at_least(pe, s_rb, n - 2)
                            for c in range(NCH):
                                last = nc.tensor.transpose(spr[o][:, c * CH:(c + 1) * CH],
                                                           sd[o][:, NCH + c:NCH + c + 1].broadcast_to([CH, C]), ident[0:CH, 0:CH])
                            last.then_inc(s_spr, 1)
                        if not (isinstance(n, int) and n >= B):
                            pe.wait_ge(s_sq, n + 1)
                            at_least(pe, s_sd, n - 1)
                            for c in range(NCH):
                                last = nc.tensor.matmul(var[par][0:CH, c:c + 1], sq[par][:, c * CH:(c + 1) * CH], mean_m[:, 0:1],
                                                        start=True, stop=True)
                            last.then_inc(s_var, 1)

                    rounds(pe, seq, B, 1)

                @block.scalar
                def _(act):
                    def seq(n, par):
                        o = 1 - par
                        if not (isinstance(n, int) and n == 0):
                            act.wait_ge(s_var, n)
                            at_least(act, s_rs, n - 2)
                            nc.scalar.activation(sd[o][:, 0:NCH], var[o][0:CH, 0:NCH], ACT.Sqrt, bias=eps[0:CH, 0:1]).then_inc(s_sd, 1)
                        if not (isinstance(n, int) and n >= B):
                            act.wait_ge(s_cen, n + 1)
                            at_least(act, s_var, n - 1)
                            nc.scalar.activation(sq[par][:, :], cen[par][:, 0:T], ACT.Square).then_inc(s_sq, 1)
                        if not (isinstance(n, int) and n == 0):
                            act.wait_ge(s_spr, n)
                            at_least(act, s_xh, n - 2)
                            nc.scalar.activation(rb[o][:, :], spr[o][:, 0:T], ACT.Copy).then_inc(s_rb, 1)

                    rounds(act, seq, B, 1)

                @block.vector
                def _(dve):
                    def apply_bn(n):
                        nc.vector.tensor_scalar(Y[:, n, :], Y[:, n, :], bn[:, 2:3], bn[:, 3:4], ALU.mult, ALU.add).then_inc(s_h, 1)

                    def seq(n, par):
                        o = 1 - par
                        if not (isinstance(n, int) and n == 0):
                            dve.wait_ge(s_sd, n)
                            at_least(dve, s_spr, n - 2)
                            nc.vector.reciprocal(sd[o][:, NCH:2 * NCH], sd[o][:, 0:NCH]).then_inc(s_rs, 1)
                        if batch_norm and not (isinstance(n, int) and n >= B):
                            apply_bn(n)
                        if not (isinstance(n, int) and n == 0):
                            dve.wait_ge(s_rb, n)
                            dve.wait_ge(s_cen, n)
                            nc.vector.tensor_tensor(XH[:, n - 1, :], cen[o][:, 0:T], rb[o][:, :], ALU.mult).then_inc(s_xh, 1)

                    rounds(dve, seq, B, 1)

        layer_norm("ln1_", True)

        with ExitStack() as p:
            pq = [[ps(f"proj{j}{i}", on=p) for i in range(2)] for j in range(3)]
            vtp = [ps(f"vt_ps{i}", on=p) for i in range(2)]
            qs = [[sb(f"qkv{j}{i}", [C, T], on=p) for i in range(2)] for j in range(3)]
            vt = [sb(f"vt{i}", [CH, NCH * C], on=p) for i in range(2)]
            s_pr = [sem(f"proj_ready{j}") for j in range(3)]
            s_ge = [sem(f"gelu_ready{j}") for j in range(3)]
            s_vt, s_vc = sem("v_transposed"), sem("v_copied")
            s_store = [sem(f"qkv_stored{i}") for i in range(2)]
            block = p.enter_context(nc.Block())

            def stored(n):
                return 48 * (n // 2)

            @block.tensor
            def _(pe):
                def seq(n, par):
                    o = 1 - par
                    live = not (isinstance(n, int) and n >= B)
                    for j in (0, 1, None, 2):
                        if j is None:
                            if not (isinstance(n, int) and n == 0):
                                pe.wait_ge(s_ge[2], n)
                                at_least(pe, s_vc, n - 2)
                                for c in range(NCH):
                                    last = nc.tensor.transpose(vtp[o][0:CH, c * C:(c + 1) * C], qs[2][o][:, c * CH:(c + 1) * CH], ident)
                                last.then_inc(s_vt, 1)
                        elif live:
                            at_least(pe, s_ge[j], n - 1)
                            nc.tensor.matmul(pq[j][par][:, 0:T], aw[:, j, :], XH[:, n, :], start=True, stop=True).then_inc(s_pr[j], 1)

                rounds(pe, seq, B, 1)

            @block.scalar
            def _(act):
                nc.scalar.preload_act_table(ACT.Gelu)

                def seq(n, par):
                    if not (isinstance(n, int) and n < 2):
                        act.wait_ge(s_store[par], stored(n))
                        act.wait_ge(s_vt, n - 1)
                    for j in range(3):
                        act.wait_ge(s_pr[j], n + 1)
                        nc.scalar.activation(qs[j][par][:, :], pq[j][par][:, 0:T], ACT.Gelu, bias=ab[:, j:j + 1]).then_inc(s_ge[j], 1)

                rounds(act, seq, B)

            @block.vector
            def _(dve):
                def seq(n, par):
                    dve.wait_ge(s_vt, n + 1)
                    if not (isinstance(n, int) and n < 2):
                        dve.wait_ge(s_store[par], stored(n))
                    nc.vector.tensor_copy(vt[par][:, :], vtp[par][0:CH, :]).then_inc(s_vc, 1)

                rounds(dve, seq, B)

            @block.sync
            def _(sp):
                def seq(n, par):
                    sp.wait_ge(s_par, 80)
                    sp.wait_ge(s_ge[0], n + 1)
                    sp.dma_start(q_d[n], qs[0][par][:, :]).then_inc(s_store[par], 16)
                    sp.wait_ge(s_par, 80)
                    sp.wait_ge(s_ge[1], n + 1)
                    sp.dma_start(k_d[n], qs[1][par][:, :]).then_inc(s_store[par], 16)
                    sp.wait_ge(s_par, 80)
                    sp.wait_ge(s_vc, n + 1)
                    sp.dma_start(v_d[n], vt[par][:, :]).then_inc(s_store[par], 16)

                rounds(sp, seq, B)
                sp.wait_ge(s_store[0], 24 * B)
                sp.wait_ge(s_store[1], 24 * B)

        with ExitStack() as p:
            qr = [sb(f"qr{i}", [C, T], on=p) for i in range(2)]
            kr = [sb(f"kr{i}", [C, T], on=p) for i in range(2)]
            vr = [sb(f"vr{i}", [CH, NCH * C], on=p) for i in range(2)]
            qm = [[sb(f"qm{i}{j}", [C, T], on=p) for j in range(2)] for i in range(2)]
            vm = [[sb(f"vm{i}{j}", [CH, NCH * C], on=p) for j in range(2)] for i in range(2)]
            vmk = sb("vmk", [CH, 2, NCH * C], on=p)
            pr = [sb(f"pr{i}", [CH, T], on=p) for i in range(3)]
            pt = [sb(f"pt{i}", [CH, T], on=p) for i in range(8)]
            nm = sb("nm", [CH, 8], on=p)
            rs = [sb(f"rs{i}", [CH, HEADS], on=p) for i in range(2)]
            ri = [sb(f"ri{i}", [CH, HEADS], on=p) for i in range(2)]
            rw = [sb(f"rw{i}", [CH, C], on=p) for i in range(2)]
            ones = sb("ones", [CH, C], on=p)
            rc = sb("rc", [C, CH], on=p)
            s_bank = [ps(f"s{i}", on=p) for i in range(3)]
            t_bank = [ps(f"t{i}", on=p) for i in range(2)]
            o_bank = [ps(f"o{i}", on=p) for i in range(2)]
            r_bank = ps("r", on=p)
            s_mk = sem("masks_loaded")
            s_ld = [sem(f"qkv_loaded{i}") for i in range(2)]
            s_mq, s_s, s_max, s_exp, s_t = sem("qv_masked"), sem("scores_ready"), sem("max_ready"), sem("exp_ready"), sem("p_transposed")
            s_ed, s_ea, s_av = sem("pt_copied_dve"), sem("pt_copied_act"), sem("av_done")
            s_rw, s_ones = sem("rinv_widened"), sem("ones_set")
            s_ri, s_r, s_rc, s_o = sem("rsum_inverted"), sem("rinv_spread"), sem("rinv_in_sbuf"), sem("o_ready")
            block = p.enter_context(nc.Block())
            NH = NCH * HEADS
            QUADS = NH // 4

            @block.sync
            def _(sp):
                sp.dma_start(vmk[:, :, :], vmask).then_inc(s_mk, 16)

                def seq(n, par):
                    if not (isinstance(n, int) and n < 2):
                        sp.wait_ge(s_par, 80)
                        sp.wait_ge(s_av, (n - 1) * QUADS)
                    sp.dma_start(qr[par][:, :], q_d[n]).then_inc(s_ld[par], 16)
                    sp.dma_start(kr[par][:, :], k_d[n]).then_inc(s_ld[par], 16)
                    sp.dma_start(vr[par][:, :], v_d[n]).then_inc(s_ld[par], 16)

                rounds(sp, seq, B)

            @block.gpsimd
            def _(pool):

                nc.gpsimd.memset(ones[:, :], 1.0).then_inc(s_ones, 1)
                pool.wait_ge(s_ones, 1)

                def mask(n, par):
                    pool.wait_ge(s_mk, 16)
                    pool.wait_ge(s_ld[par], 48 * (n // 2 + 1))
                    if not (isinstance(n, int) and n < 2):
                        pool.wait_ge(s_av, (n - 1) * QUADS)
                    for j in range(2):
                        nc.gpsimd.tensor_tensor(qm[par][j][:, :], qr[par][:, :], par_m[:, j:j + 1].broadcast_to([C, T]), ALU.mult).then_inc(s_mq, 1)
                    for j in range(2):
                        nc.gpsimd.tensor_tensor(vm[par][j][:, :], vr[par][:, :], vmk[:, j, :], ALU.mult).then_inc(s_mq, 1)

                def seq(n, par):
                    for c in range(NCH):
                        u = n * NCH + c
                        pool.wait_ge(s_mk, 16)
                        pool.wait_ge(s_ri, u + 1)
                        at_least(pool, s_r, u - 1)
                        wide = ri[c % 2][:, :].rearrange("p (h o) -> p h o", o=1).broadcast_to([CH, HEADS, HD])
                        nc.gpsimd.tensor_tensor(rw[c % 2][:, :].rearrange("p (h d) -> p h d", d=HD), wide,
                                                ones[:, :].rearrange("p (h d) -> p h d", d=HD), ALU.mult).then_inc(s_rw, 1)
                        if c == 0 and not (isinstance(n, int) and n == B - 1):
                            mask(n + 1, 1 - par)

                mask(0, 0)
                seq(0, 0)
                seq(1, 1)
                with pool.Fori(1, B // 2 - 1) as n:
                    seq(2 * n, 0)
                    seq(2 * n + 1, 1)
                seq(B - 2, 0)
                seq(B - 1, 1)

            def place(i):
                return i // HEADS, i // 4 % 2, i % 4

            @block.tensor
            def _(pe):
                def scores(n, i, par):
                    c, j, quad = place(i)
                    g = n * NH + i
                    if i == 0:
                        pe.wait_ge(s_ld[par], 48 * (n // 2 + 1))
                        pe.wait_ge(s_mq, 4 * n + 4)
                    at_least(pe, s_exp, g - 1)
                    rows = slice(32 * quad, 32 * quad + 32)
                    nc.tensor.matmul(s_bank[i % 2][0:CH, 0:T], qm[par][j][rows, c * CH:(c + 1) * CH], kr[par][rows, :],
                                     start=True, stop=True).then_inc(s_s, 1)

                def seq(n, par):
                    for i in range(NH):
                        c, j, quad = place(i)
                        g, u = n * NH + i, n * NCH + c
                        if i + 1 < NH:
                            scores(n, i + 1, par)
                        elif not (isinstance(n, int) and n == B - 1):
                            scores(n + 1, 0, 1 - par)
                        pe.wait_ge(s_exp, g + 1)
                        h2 = n * (NH // 2) + i // 2
                        at_least(pe, s_ea if i % 2 else s_ed, h2)
                        for k in range(NCH):
                            last = nc.tensor.transpose(t_bank[i % 2][0:CH, k * CH:(k + 1) * CH], pr[i % 2][:, k * CH:(k + 1) * CH],
                                                       ident[0:CH, 0:CH])
                        last.then_inc(s_t, 1)
                        if quad == 3:
                            pe.wait_ge(s_ed, h2 + 1)
                            pe.wait_ge(s_ea, h2 + 1)
                            if j == 0:
                                at_least(pe, s_o, u - 1)
                            for k in range(NCH):
                                for q in range(4):
                                    last = nc.tensor.matmul(o_bank[c % 2][32 * q:32 * q + 32, 0:CH],
                                                            vm[par][j][:, k * C + 32 * q:k * C + 32 * q + 32],
                                                            pt[4 * j + q][:, k * CH:(k + 1) * CH],
                                                            start=j == 0 and k == 0, stop=j == 1 and k == NCH - 1)
                            last.then_inc(s_av, 1)
                            if j == 1:
                                pe.wait_ge(s_rw, u + 1)
                                at_least(pe, s_rc, u)
                                nc.tensor.transpose(r_bank[:, 0:CH], rw[c % 2][:, :], ident[0:CH, 0:CH]).then_inc(s_r, 1)

                scores(0, 0, 0)
                seq(0, 0)
                seq(1, 1)
                with pe.Fori(1, B // 2 - 1) as n:
                    seq(2 * n, 0)
                    seq(2 * n + 1, 1)
                seq(B - 2, 0)
                seq(B - 1, 1)

            @block.scalar
            def _(act):
                nc.scalar.preload_act_table(ACT.Exp)

                def copy_pt(n, i):
                    g = n * NH + i
                    act.wait_ge(s_t, g + 1)
                    at_least(act, s_av, n * QUADS + i // 4 - 1)
                    nc.scalar.activation(pt[i % 8][:, :], t_bank[i % 2][0:CH, 0:T], ACT.Copy).then_inc(s_ea, 1)

                def copy_rc(u):
                    act.wait_ge(s_r, u + 1)
                    at_least(act, s_o, u)
                    nc.scalar.activation(rc[:, :], r_bank[:, 0:CH], ACT.Copy).then_inc(s_rc, 1)

                def seq(n, par):
                    for i in range(NH):
                        c, j, quad = place(i)
                        g, u = n * NH + i, n * NCH + c
                        act.wait_ge(s_max, g + 1)
                        at_least(act, s_t, g - 1)
                        if i % HEADS == 0:
                            at_least(act, s_ri, u - 1)
                        nc.scalar.activation(pr[i % 2][:, :], s_bank[i % 2][0:CH, 0:T], ACT.Exp, bias=nm[:, i % 8:i % 8 + 1],
                                             accum_out=rs[c % 2][:, i % 8:i % 8 + 1]).then_inc(s_exp, 1)
                        if i % 2 == 0 and not (isinstance(n, int) and g == 0):
                            copy_pt(n - 1 if i == 0 else n, (i - 1) % NH)
                        if i % HEADS == 2 and not (isinstance(n, int) and u == 0):
                            copy_rc(u - 1)

                rounds(act, seq, B)
                copy_pt(B - 1, NH - 1)
                copy_rc(B * NCH - 1)

            @block.vector
            def _(dve):
                def row_max(n, i):
                    g = n * NH + i
                    dve.wait_ge(s_s, g + 1)
                    at_least(dve, s_exp, g - 7)
                    nc.vector.tensor_reduce(nm[:, i % 8:i % 8 + 1], s_bank[i % 2][0:CH, 0:T], AX, ALU.max, negate=True).then_inc(s_max, 1)

                def finish(n, c):
                    u = n * NCH + c
                    dve.wait_ge(s_rc, u + 1)
                    dve.wait_ge(s_av, 2 * u + 2)
                    nc.vector.tensor_tensor(XH[:, n, c * CH:(c + 1) * CH], o_bank[c % 2][:, 0:CH], rc[:, :], ALU.mult).then_inc(s_o, 1)

                def seq(n, par):
                    for i in range(NH):
                        c, j, quad = place(i)
                        g, u = n * NH + i, n * NCH + c
                        if i + 1 < NH:
                            row_max(n, i + 1)
                        elif not (isinstance(n, int) and n == B - 1):
                            row_max(n + 1, 0)
                        if i % 2 == 0:
                            dve.wait_ge(s_t, g + 1)
                            at_least(dve, s_av, n * QUADS + i // 4 - 1)
                            nc.vector.tensor_copy(pt[i % 8][:, :], t_bank[0][0:CH, 0:T]).then_inc(s_ed, 1)
                        if i % HEADS == HEADS - 1:
                            dve.wait_ge(s_exp, g + 1)
                            at_least(dve, s_rw, u - 1)
                            nc.vector.reciprocal(ri[c % 2][:, :].rearrange("p (q j) -> p j q", j=2),
                                                 rs[c % 2][:, :].rearrange("p (j q) -> p j q", j=2)).then_inc(s_ri, 1)
                        if i % HEADS == 4 and not (isinstance(n, int) and u == 0):
                            finish(n - 1 if c == 0 else n, (c - 1) % NCH)

                row_max(0, 0)
                seq(0, 0)
                seq(1, 1)
                with dve.Fori(1, B // 2 - 1) as n:
                    seq(2 * n, 0)
                    seq(2 * n + 1, 1)
                seq(B - 2, 0)
                seq(B - 1, 1)
                finish(B - 1, NCH - 1)

        with ExitStack() as p:
            wps = [ps(f"wo_ps{i}", on=p) for i in range(2)]
            gb = [sb(f"gb{i}", [C, T], on=p) for i in range(2)]
            s_wo, s_go, s_add = sem("wo_ready"), sem("wo_gelu"), sem("residual_added")
            block = p.enter_context(nc.Block())

            @block.tensor
            def _(pe):
                def seq(n, par):
                    at_least(pe, s_go, n - 1)
                    nc.tensor.matmul(wps[par][:, 0:T], aw[:, 3, :], XH[:, n, :], start=True, stop=True).then_inc(s_wo, 1)

                rounds(pe, seq, B)

            @block.scalar
            def _(act):
                nc.scalar.preload_act_table(ACT.Gelu)

                def seq(n, par):
                    act.wait_ge(s_wo, n + 1)
                    at_least(act, s_add, n - 1)
                    nc.scalar.activation(gb[par][:, :], wps[par][:, 0:T], ACT.Gelu, bias=ab[:, 3:4]).then_inc(s_go, 1)

                rounds(act, seq, B)

            @block.vector
            def _(dve):
                def seq(n, par):
                    dve.wait_ge(s_go, n + 1)
                    nc.vector.tensor_tensor(Y[:, n, :], Y[:, n, :], gb[par][:, :], ALU.add).then_inc(s_add, 1)

                rounds(dve, seq, B)

        layer_norm("ln2_", False)

        with ExitStack() as p:
            GW = 4 * C
            wx, wh = sb("wx", [C, S, GW], on=p), sb("wh", [C, S, GW], on=p)
            wl = sb("wl", [C, 3, S], on=p)
            rows = 3 * S
            bi, bh = sb("bi", [rows, GW + S], on=p), sb("bh", [rows, GW + S], on=p)
            bsplit = [sb(f"bsplit{i}", [rows, GW + S], bf16, on=p) for i in range(3)]
            bw = sb("bw", [rows, GW + S], bf16, on=p)
            ind = sb("ind", [rows, C], bf16, on=p)
            xs = sb("xs", [C, STEPS, S, B], on=p)
            hs = sb("hs", [C, STEPS, B], on=p)
            ct = sb("ct", [C, B], on=p)
            ob = [sb(f"ob{i}", [C, 4, B], on=p) for i in range(4)]
            fi = [sb(f"fi{i}", [C, 2 * C], on=p) for i in range(2)]
            tg = [sb(f"tg{i}", [C, C], on=p) for i in range(2)]
            to = [sb(f"to{i}", [C, C], on=p) for i in range(2)]
            tc = [sb(f"tc{i}", [C, C], on=p) for i in range(2)]
            uu, vv = sb("uu", [C, C], on=p), sb("vv", [C, C], on=p)
            c2 = [sb(f"c2{i}", [C, C], on=p) for i in range(2)]
            h2 = [sb(f"h2{i}", [C, C], on=p) for i in range(2)]
            lm, lq, le = sb("lm", [C, 1], on=p), sb("lq", [C, 1], on=p), sb("le", [C, S], on=p)
            sel = [sb(f"sel{i}", [C, C], on=p) for i in range(2)]
            zero = sb("zero", [C, B], on=p)
            g_fi = [ps(f"g_fi{i}", on=p) for i in range(2)]
            g_g = [ps(f"g_g{i}", on=p) for i in range(2)]
            g_o = [ps(f"g_o{i}", on=p) for i in range(2)]
            hc, cl = ps("hc", on=p), ps("cl", on=p)
            s_w, s_sc, s_bz = sem("lstm_loaded"), sem("lstm_scaled"), sem("bias_chain")
            s_z = sem("state_zeroed")
            s_xs, s_xu = sem("x_staged"), sem("x_used")
            s_l, s_fi, s_g, s_go2 = sem("logits_ready"), sem("fi_ready"), sem("g_ready"), sem("o_gate_ready")
            s_tfi, s_tg, s_to, s_tc = sem("fi_tanh"), sem("g_tanh"), sem("o_tanh"), sem("c_tanh")
            s_m, s_q, s_sel = sem("logit_max"), sem("chosen"), sem("sel_ready")
            s_u, s_v, s_c2, s_h2 = sem("u_ready"), sem("v_ready"), sem("c2_ready"), sem("h2_ready")
            s_ctp, s_ctc, s_crep = sem("cT_ready"), sem("cT_copied"), sem("crep_ready")
            s_htp, s_htc = sem("hT_ready"), sem("hT_copied")
            s_ob, s_out = sem("out_ready"), [sem(f"out_stored{i}") for i in range(4)]
            block = p.enter_context(nc.Block())
            FI, G, O, L = slice(0, 2 * C), slice(2 * C, 3 * C), slice(3 * C, 4 * C), slice(4 * C, 4 * C + S)
            NB = T // STEPS
            QS = STEPS // 4

            @block.sync
            def _(sp):
                sp.dma_start(wx[:, :, :], w_ih).then_inc(s_w, 16)
                sp.dma_start(wh[:, :, :], w_hh).then_inc(s_w, 16)
                sp.dma_start(wl[:, :, :], w_sel).then_inc(s_w, 16)
                for k in range(3):
                    sp.dma_start(bi[k * S:(k + 1) * S, 0:GW], b_ih).then_inc(s_w, 16)
                    sp.dma_start(bh[k * S:(k + 1) * S, 0:GW], b_hh).then_inc(s_w, 16)
                    sp.dma_start(bi[k * S:(k + 1) * S, GW:GW + S], b_sel).then_inc(s_w, 16)

                def body(it, first):
                    for q in range(QS):
                        sp.wait_ge(s_par, 80)
                        sp.wait_ge(s_ob, it * QS + q + 1)
                        sp.dma_start(out[:, bass.ds(it * STEPS + 4 * q, 4), :], ob[q][:, :, :]).then_inc(s_out[q], 16)

                body(0, True)
                with sp.Fori(1, NB) as it:
                    body(it, False)
                for q in range(QS):
                    sp.wait_ge(s_out[q], 16 * NB)

            @block.gpsimd
            def _(pool):
                def stage(it, q, first):
                    pool.wait_ge(s_par, 80)
                    if not first:
                        pool.wait_ge(s_xu, (it - 1) * STEPS + 4 * q + 4)
                    for s in range(S):
                        last = nc.gpsimd.tensor_copy(xs[:, 4 * q:4 * q + 4, s, :],
                                                     XH[:, :, bass.ds(it * STEPS + 4 * q, 4)].rearrange("p b t -> p t b"))
                    last.then_inc(s_xs, 1)

                def body(it, first, last):
                    for q in range(QS):
                        if not last:
                            stage(it + 1, q, False)
                        pool.wait_ge(s_htc, it * STEPS + 4 * q + 4)
                        if not first:
                            pool.wait_ge(s_out[q], it * 16)
                        nc.gpsimd.tensor_tensor(ob[q][:, :, :], hs[:, 4 * q:4 * q + 4, :],
                                                Y[:, :, bass.ds(it * STEPS + 4 * q, 4)].rearrange("p b t -> p t b"),
                                                ALU.add).then_inc(s_ob, 1)

                for q in range(QS):
                    stage(0, q, True)
                body(0, True, False)
                with pool.Fori(1, NB - 1) as it:
                    body(it, False, False)
                body(NB - 1, False, True)

            @block.tensor
            def _(pe):
                pe.wait_ge(s_w, 16 * 12)
                pe.wait_ge(s_sc, 4)
                pe.wait_ge(s_z, 1)

                def logits(state, which, stop):
                    for s in range(S):
                        last = nc.tensor.matmul(cl[32 * s:32 * s + 32, C:C + S], state, wl[:, which, :], start=False, stop=stop, skip_group_check=True)
                    return last

                def x_part(bank, cols, k):
                    n = cols.stop - cols.start
                    for s in range(S):
                        nc.tensor.matmul(bank[32 * s:32 * s + 32, 0:n], xs[:, k, 0, :], wx[:, s, cols], start=True, stop=False, skip_group_check=True)
                    return nc.tensor.matmul(bank[:, 0:n], ind[:, :], bw[:, cols], start=False, stop=False, skip_group_check=True)

                def h_part(bank, cols, hk):
                    n = cols.stop - cols.start
                    for s in range(S):
                        last = nc.tensor.matmul(bank[32 * s:32 * s + 32, 0:n], hk, wh[:, s, cols], start=False, stop=True, skip_group_check=True)
                    return last

                def logits_x(k):
                    nc.tensor.matmul(cl[:, C:C + S], xs[:, k, :, :].rearrange("p s b -> p (s b)"), wl[:, 2, :], start=True, stop=False, skip_group_check=True)
                    nc.tensor.matmul(cl[:, C:C + S], ind[:, :], bw[:, L], start=False, stop=False, skip_group_check=True)

                def step(t, k, first, last):
                    par = k % 2
                    hk = zero[:, :] if first else hs[:, (k - 1) % STEPS, :]
                    ck = zero[:, :] if first else ct[:, :]
                    if not first:
                        pe.wait_ge(s_ctc, t)
                    logits(ck, 1, False)
                    if not first:
                        pe.wait_ge(s_htc, t)
                    h_part(g_fi[par], FI, hk).then_inc(s_fi, 1)
                    h_part(g_g[par], G, hk).then_inc(s_g, 1)
                    logits(hk, 0, True).then_inc(s_l, 1)
                    h_part(g_o[par], O, hk).then_inc(s_go2, 1)
                    nk = (k + 1) % STEPS
                    if not last:
                        if nk % 4 == 0:
                            pe.wait_ge(s_xs, (t + 1) // 4 + 1 if isinstance(t, int) else t4(t, k) + 1)
                        at_least(pe, s_tfi, t)
                        x_part(g_fi[1 - par], FI, nk)
                        at_least(pe, s_tg, t)
                        x_part(g_g[1 - par], G, nk)
                    pe.wait_ge(s_sel, t + 1)
                    pe.wait_ge(s_c2, t + 1)
                    nc.tensor.matmul(hc[:, 0:B], c2[par][:, :], sel[par][:, 0:B], start=True, stop=True).then_inc(s_ctp, 1)
                    pe.wait_ge(s_h2, t + 1)
                    pe.wait_ge(s_ctc, t + 1)
                    nc.tensor.matmul(hc[:, B:2 * B], h2[par][:, :], sel[par][:, 0:B], start=True, stop=True).then_inc(s_htp, 1)
                    if not last:
                        nc.tensor.matmul(cl[:, 0:C], sel[par][:, :], c2[par][:, :], start=True, stop=True).then_inc(s_crep, 1)
                        logits_x(nk)
                        at_least(pe, s_to, t)
                        x_part(g_o[1 - par], O, nk).then_inc(s_xu, 1)

                t4_base = {}

                def t4(t, k):
                    return t4_base["it"] * QS + (k + 1) // 4

                def body(it, first, last):
                    t4_base["it"] = it
                    for k in range(STEPS):
                        step(it * STEPS + k, k, first and k == 0, last and k == STEPS - 1)

                pe.wait_ge(s_xs, 1)
                x_part(g_fi[0], FI, 0)
                x_part(g_g[0], G, 0)
                logits_x(0)
                x_part(g_o[0], O, 0).then_inc(s_xu, 1)
                body(0, True, False)
                with pe.Fori(1, NB - 1) as it:
                    body(it, False, False)
                body(NB - 1, False, True)

            @block.scalar
            def _(act):
                nc.scalar.preload_act_table(ACT.Tanh)

                def step(t, k):
                    par = k % 2
                    act.wait_ge(s_fi, t + 1)
                    at_least(act, s_u, t - 1)
                    at_least(act, s_v, t - 1)
                    nc.scalar.activation(fi[par][:, :], g_fi[par][:, 0:2 * C], ACT.Tanh).then_inc(s_tfi, 1)
                    act.wait_ge(s_g, t + 1)
                    nc.scalar.activation(tg[par][:, :], g_g[par][:, 0:C], ACT.Tanh).then_inc(s_tg, 1)
                    act.wait_ge(s_go2, t + 1)
                    at_least(act, s_h2, t - 1)
                    nc.scalar.activation(to[par][:, :], g_o[par][:, 0:C], ACT.Tanh).then_inc(s_to, 1)
                    act.wait_ge(s_c2, t + 1)
                    nc.scalar.activation(tc[par][:, :], c2[par][:, :], ACT.Tanh, scale=0.5).then_inc(s_tc, 1)

                def body(it):
                    for k in range(STEPS):
                        step(it * STEPS + k, k)

                body(0)
                with act.Fori(1, NB) as it:
                    body(it)

            @block.vector
            def _(dve):
                nc.vector.memset(zero[:, :], 0.0).then_inc(s_z, 1)
                dve.wait_ge(s_w, 16 * 12)
                for w in (wx, wh):
                    nc.vector.tensor_scalar(w[:, :, FI], w[:, :, FI], 0.5, None, ALU.mult).then_inc(s_bz, 1)
                    nc.vector.tensor_scalar(w[:, :, O], w[:, :, O], 0.5, None, ALU.mult).then_inc(s_bz, 1)
                nc.vector.tensor_copy(ind[:, :], kc[0:rows, COLS[K_IND]:COLS[K_IND] + C]).then_inc(s_bz, 1)
                nc.vector.tensor_tensor(bi[:, 0:GW], bi[:, 0:GW], bh[:, 0:GW], ALU.add).then_inc(s_bz, 1)
                dve.wait_ge(s_bz, 6)
                nc.vector.tensor_scalar(bi[:, FI], bi[:, FI], 0.5, None, ALU.mult).then_inc(s_bz, 1)
                nc.vector.tensor_scalar(bi[:, O], bi[:, O], 0.5, None, ALU.mult).then_inc(s_bz, 1)
                dve.wait_ge(s_bz, 8)
                nc.vector.tensor_copy(bsplit[0][:, :], bi[:, :]).then_inc(s_bz, 1)
                dve.wait_ge(s_bz, 9)
                nc.vector.tensor_tensor(bi[:, :], bi[:, :], bsplit[0][:, :], ALU.subtract).then_inc(s_bz, 1)
                dve.wait_ge(s_bz, 10)
                nc.vector.tensor_copy(bsplit[1][:, :], bi[:, :]).then_inc(s_bz, 1)
                dve.wait_ge(s_bz, 11)
                nc.vector.tensor_tensor(bi[:, :], bi[:, :], bsplit[1][:, :], ALU.subtract).then_inc(s_bz, 1)
                dve.wait_ge(s_bz, 12)
                nc.vector.tensor_copy(bsplit[2][:, :], bi[:, :]).then_inc(s_bz, 1)
                part = kc[0:rows, COLS[K_PART]:COLS[K_PART] + 3]
                nc.vector.tensor_scalar(bw[:, :], bsplit[0][:, :], part[:, 0:1], None, ALU.mult).then_inc(s_bz, 1)
                dve.wait_ge(s_bz, 14)
                for k in (1, 2):
                    nc.vector.scalar_tensor_tensor(bw[:, :], bsplit[k][:, :], part[:, k:k + 1], bw[:, :], ALU.mult, ALU.add).then_inc(s_bz, 1)
                    dve.wait_ge(s_bz, 14 + k)
                nc.vector.engine_nop().then_inc(s_sc, 4)

                def step(t, k, first, last):
                    par = k % 2
                    dve.wait_ge(s_l, t + 1)
                    if first:
                        nc.vector.memset(vv[:, :], 0.0).then_inc(s_v, 1)
                        dve.wait_ge(s_v, 1)
                        dve.wait_ge(s_tfi, 1)
                    else:
                        dve.wait_ge(s_tfi, t + 1)
                        dve.wait_ge(s_crep, t)
                        nc.vector.scalar_tensor_tensor(vv[:, :], fi[par][:, 0:C], 1.0, cl[:, 0:C], ALU.add, ALU.mult).then_inc(s_v, 1)
                    dve.wait_ge(s_tg, t + 1)
                    nc.vector.scalar_tensor_tensor(uu[:, :], fi[par][:, C:2 * C], 1.0, tg[par][:, :], ALU.add, ALU.mult).then_inc(s_u, 1)
                    if not first:
                        nc.vector.tensor_reduce(lm[:, :], cl[:, C:C + S], AX, ALU.max).then_inc(s_m, 1)
                    dve.wait_ge(s_u, t + 1)
                    nc.vector.tensor_tensor(c2[par][:, :], uu[:, :], vv[:, :], ALU.add).then_inc(s_c2, 1)
                    if first:
                        nc.vector.tensor_copy(sel[par][:, :], const(K_SEL0)).then_inc(s_sel, 1)
                    else:
                        dve.wait_ge(s_m, t)
                        nc.vector.scalar_tensor_tensor(le[:, :], cl[:, C:C + S], lm[:, 0:1], first_w, ALU.is_ge, ALU.mult,
                                                       accum_out=lq[:, :]).then_inc(s_q, 1)
                        dve.wait_ge(s_q, t)
                        nc.vector.tensor_scalar(sel[par][:, :], pick, lq[:, 0:1], 0.0, ALU.mult, ALU.max).then_inc(s_sel, 1)
                    dve.wait_ge(s_ctp, t + 1)
                    nc.vector.tensor_copy(ct[:, :], hc[:, 0:B]).then_inc(s_ctc, 1)
                    dve.wait_ge(s_tc, t + 1)
                    dve.wait_ge(s_to, t + 1)
                    nc.vector.scalar_tensor_tensor(h2[par][:, :], to[par][:, :], 1.0, tc[par][:, :], ALU.add, ALU.mult).then_inc(s_h2, 1)
                    dve.wait_ge(s_htp, t + 1)
                    if not (isinstance(t, int) and t < STEPS):
                        if k % 4 == 0:
                            dve.wait_ge(s_ob, out_turn["it"] * QS + k // 4 - QS + 1)
                    nc.vector.tensor_copy(hs[:, k, :], hc[:, B:2 * B]).then_inc(s_htc, 1)

                out_turn = {}

                def body(it, first):
                    out_turn["it"] = it
                    for k in range(STEPS):
                        step(it * STEPS + k, k, first and k == 0, False)

                body(0, True)
                with dve.Fori(1, NB) as it:
                    body(it, False)


def constants():
    import numpy as np
    k = np.zeros((128, COLS[-1]), np.float32)
    p = np.arange(128)

    def put(which, a):
        k[:a.shape[0], COLS[which]:COLS[which] + a.shape[1]] = a

    same = (p[:, None] % 32 == p[None, :] % 32).astype(np.float32)
    put(K_ID, np.eye(128, dtype=np.float32))
    put(K_PICK, 0.5 * same)
    put(K_CENTRE, np.eye(128, dtype=np.float32) - np.float32(1 / 128))
    put(K_MEAN, np.full((128, 128), 1 / 128, np.float32))
    module, s = p[:, None] // 32, np.arange(S)[None, :]
    put(K_FIRST, np.where(s == module, 1, np.where(s < module, -8, 0)).astype(np.float32))
    put(K_PAR, np.stack([(p // 16 % 2 == j) * 0.25 for j in range(2)], 1).astype(np.float32))
    put(K_IND, (np.arange(3 * S)[:, None] % S == p[None, :] // 32).astype(np.float32))
    put(K_PART, (np.arange(3 * S)[:, None] // S == np.arange(3)[None, :]).astype(np.float32))
    put(K_SEL0, 0.5 * same * (p[:, None] < 32))
    col = np.arange(4 * 128) % 128 // 16 % 2
    vmask = np.broadcast_to(np.stack([col == j for j in range(2)]).astype(np.float32), (CH, 2, 512)).copy()
    return k, vmask


def kernel(**inputs):
    import numpy as np
    import concourse.bacc as bacc
    from concourse.bass_utils import run_bass_kernel_spmd

    a = {k: np.asarray(v) for k, v in inputs.items()}
    gates = [1, 0, 2, 3]

    def lstm_w(w):
        return w.reshape(S, 4, C, C)[:, gates].reshape(S, 4 * C, C).transpose(2, 0, 1)

    def lstm_b(b):
        return b.reshape(S, 4, C)[:, gates].reshape(S, 4 * C)

    tok = a["L0_tok_W"].T
    tokw = np.zeros((128, 3, C), np.float32)
    tokw[:, 0], tokw[:, 1], tokw[:D, 2] = tok[0:128], tok[128:256], tok[256:320]
    consts, vmask = constants()
    data = {
        "x": a["x"].transpose(2, 0, 1).reshape(D, B * T_IN),
        "tok_w": tokw,
        "tok_v": np.stack([a["L0_tok_b"], a["L0_tok_gamma"], a["L0_tok_beta"]], 1),
        "attn_w": np.stack([a[f"L0_attn_W{n}"].T for n in "qkvo"], 1),
        "attn_b": np.stack([a[f"L0_attn_b{n}"] for n in "qkvo"], 1),
        "w_ih": lstm_w(a["L0_ffn_W_ih"]),
        "w_hh": lstm_w(a["L0_ffn_W_hh"]),
        "w_sel": a["L0_ffn_W_sel"].reshape(S, 3, C).transpose(2, 1, 0),
        "b_ih": lstm_b(a["L0_ffn_b_ih"]),
        "b_hh": lstm_b(a["L0_ffn_b_hh"]),
        "b_sel": np.broadcast_to(a["L0_ffn_b_sel"], (S, S)),
        "consts": consts,
        "vmask": vmask,
    }
    nc = bacc.Bacc("TRN2", target_bir_lowering=False, num_devices=1)
    arrays, args = {}, []
    for name, v in data.items():
        v = np.ascontiguousarray(v)
        arrays[name + "_dram"] = v
        args.append(nc.dram_tensor(name + "_dram", v.shape, mybir.dt.from_np(v.dtype), kind="ExternalInput").ap())
    out = nc.dram_tensor("out_dram", (C, T, B), mybir.dt.float32, kind="ExternalOutput").ap()
    audio_tower(nc, *args, out)
    r = run_bass_kernel_spmd(nc, [arrays], core_ids=[0])
    return np.ascontiguousarray(np.asarray(r.results[0]["out_dram"]).transpose(2, 1, 0))
```

```python
import concourse.bass as bass
from concourse import mybir
from contextlib import ExitStack

B, T_IN, D, TAPS = 32, 500, 64, 5
T = T_IN - TAPS + 1
C = 128
HEADS, HD = 8, 16
CH = 124
NCH = T // CH
S = 4
EPS = 1e-5
STEPS = 16
PIECES = 4

K_ID, K_PICK, K_CENTRE, K_MEAN, K_FIRST, K_PAR, K_IND, K_PART, K_SEL0 = range(9)
WIDTHS = [C, C, C, C, S, 2, C, 3, C]
COLS = [sum(WIDTHS[:n]) for n in range(len(WIDTHS) + 1)]


def audio_tower(nc, x, tok_w, tok_v, attn_w, attn_b, w_ih, w_hh, w_selc, b_ih, b_hh, consts, vmask, out):
    f32, bf16 = mybir.dt.float32, mybir.dt.bfloat16
    ALU, ACT = mybir.AluOpType, mybir.ActivationFunctionType
    AX = mybir.AxisListType.X

    def at_least(eng, sem, n):
        if not (isinstance(n, int) and n <= 0):
            eng.wait_ge(sem, n)

    def rounds(eng, body, total, tail=0):
        body(0, 0)
        body(1, 1)
        with eng.Fori(1, total // 2) as i:
            body(2 * i, 0)
            body(2 * i + 1, 1)
        for n in range(total, total + tail):
            body(n, n % 2)

    stack = ExitStack()
    with stack:
        def sb(name, shape, dt=f32, on=stack):
            return on.enter_context(nc.sbuf_tensor(name, shape, dt))

        def ps(name, on=stack):
            return on.enter_context(nc.psum_tensor(name, [128, 512], f32))

        def sem(name):
            return stack.enter_context(nc.semaphore(name))

        Y = sb("Y", [C, B, T])
        X = sb("X", [C, B * T_IN])
        XH = X[:, 0:B * T].rearrange("p (b t) -> p b t", b=B)
        kc = sb("kc", [128, COLS[-1]])

        def const(k):
            return kc[:, COLS[k]:COLS[k] + WIDTHS[k]]

        ident, pick, centre, mean_m, first_w, par_m = (const(k) for k in range(6))
        tokw = sb("tokw", [128, 3, C])
        tokv = sb("tokv", [C, 3])
        bn = sb("bn", [C, 4])
        eps = sb("eps", [128, 1])
        aw = sb("aw", [C, 4, C])
        ab = sb("ab", [C, 4])
        q_d = nc.dram_tensor("q_scratch", [B, C, T], f32, kind="Internal").ap()
        k_d = nc.dram_tensor("k_scratch", [B, C, T], f32, kind="Internal").ap()
        v_d = nc.dram_tensor("v_scratch", [B, CH, NCH * C], f32, kind="Internal").ap()

        with ExitStack() as p:
            stats = sb("stats", [C, B, 6], on=p)
            mv = sb("mv", [C, 2], on=p)
            cps = [ps(f"conv{i}", on=p) for i in range(2)]
            s_par, s_eps = sem("params_loaded"), sem("eps_set")
            s_x = [sem(f"x_loaded{i}") for i in range(PIECES)]
            s_conv, s_relu, s_st = sem("conv_ready"), sem("relu_ready"), sem("stats_ready")
            s_mv, s_std, s_bn = sem("bn_moments"), sem("bn_std"), sem("bn_chain")
            block = p.enter_context(nc.Block())
            half = B * T_IN // PIECES

            @block.sync
            def _(sp):
                sp.dma_start(tokw[:, :, :], tok_w).then_inc(s_par, 16)
                sp.dma_start(tokv[:, :], tok_v).then_inc(s_par, 16)
                for i in range(PIECES):
                    n = min(half, B * T_IN - 1 - i * half)
                    sp.dma_start(X[0:D, i * half:(i + 1) * half], x[:, i * half:(i + 1) * half]).then_inc(s_x[i], 16)
                    sp.dma_start(X[D:2 * D, i * half:i * half + n], x[:, i * half + 1:i * half + 1 + n]).then_inc(s_x[i], 16)
                sp.dma_start(kc[:, :], consts).then_inc(s_par, 16)
                sp.dma_start(aw[:, :, :], attn_w).then_inc(s_par, 16)
                sp.dma_start(ab[:, :], attn_b).then_inc(s_par, 16)
                sp.wait_ge(s_par, 80)

            @block.tensor
            def _(pe):
                pe.wait_ge(s_par, 80)

                def seq(n, par):
                    at_least(pe, s_relu, n - 1)
                    at = n * T_IN
                    nc.tensor.matmul(cps[par][:, 0:T], tokw[:, 0, :], X[:, bass.ds(at, T)], start=True, stop=False)
                    nc.tensor.matmul(cps[par][:, 0:T], tokw[:, 1, :], X[:, bass.ds(at + 2, T)], start=False, stop=False)
                    nc.tensor.matmul(cps[par][:, 0:T], tokw[0:D, 2, :], X[0:D, bass.ds(at + 4, T)],
                                     start=False, stop=True).then_inc(s_conv, 1)

                each = B // PIECES
                for i in range(PIECES):
                    pe.wait_ge(s_x[i], 32)
                    if i + 1 < PIECES:
                        pe.wait_ge(s_x[i + 1], 32)
                    if i == 0:
                        seq(0, 0)
                        seq(1, 1)
                    with pe.Fori(i * each // 2 + (1 if i == 0 else 0), (i + 1) * each // 2) as n:
                        seq(2 * n, 0)
                        seq(2 * n + 1, 1)

            @block.scalar
            def _(act):
                act.wait_ge(s_par, 80)

                def seq(n, par):
                    act.wait_ge(s_conv, n + 1)
                    nc.scalar.activation(Y[:, n, :], cps[par][:, 0:T], ACT.Relu, bias=tokv[:, 0:1]).then_inc(s_relu, 1)

                rounds(act, seq, B)
                act.wait_ge(s_mv, 1)
                act.wait_ge(s_eps, 1)
                nc.scalar.activation(bn[:, 0:1], mv[:, 1:2], ACT.Sqrt, bias=eps[:, 0:1]).then_inc(s_std, 1)

            @block.vector
            def _(dve):
                nc.vector.memset(eps[:, :], EPS).then_inc(s_eps, 1)

                def seq(n, par):
                    dve.wait_ge(s_relu, n + 1)
                    nc.vector.bn_stats(stats[:, n, :], Y[:, n, :]).then_inc(s_st, 1)

                rounds(dve, seq, B)
                dve.wait_ge(s_st, B)
                nc.vector.bn_aggr(mv[:, :], stats[:, :, :].rearrange("p b s -> p (b s)")).then_inc(s_mv, 1)
                dve.wait_ge(s_std, 1)
                nc.vector.reciprocal(bn[:, 1:2], bn[:, 0:1]).then_inc(s_bn, 1)
                dve.wait_ge(s_bn, 1)
                nc.vector.tensor_tensor(bn[:, 2:3], bn[:, 1:2], tokv[:, 1:2], ALU.mult).then_inc(s_bn, 1)
                dve.wait_ge(s_bn, 2)
                nc.vector.tensor_tensor(bn[:, 3:4], mv[:, 0:1], bn[:, 2:3], ALU.mult).then_inc(s_bn, 1)
                dve.wait_ge(s_bn, 3)
                nc.vector.tensor_tensor(bn[:, 3:4], tokv[:, 2:3], bn[:, 3:4], ALU.subtract).then_inc(s_bn, 1)

        def layer_norm(tag, batch_norm):
            with ExitStack() as p:
                sq = [sb(f"{tag}sq{i}", [C, T], on=p) for i in range(2)]
                rb = [sb(f"{tag}rb{i}", [C, T], on=p) for i in range(2)]
                sd = [sb(f"{tag}sd{i}", [CH, 2 * NCH], on=p) for i in range(2)]
                cen = [ps(f"{tag}cen{i}", on=p) for i in range(2)]
                var = [ps(f"{tag}var{i}", on=p) for i in range(2)]
                spr = [ps(f"{tag}spr{i}", on=p) for i in range(2)]
                s_h, s_cen, s_sq, s_var = (sem(tag + n) for n in ("h_ready", "centred", "squared", "var_ready"))
                s_sd, s_rs, s_spr, s_rb, s_xh = (sem(tag + n) for n in ("std_ready", "rstd_ready", "spread", "rstd_in_sbuf", "xhat_ready"))
                block = p.enter_context(nc.Block())

                @block.tensor
                def _(pe):
                    def seq(n, par):
                        o = 1 - par
                        if not (isinstance(n, int) and n >= B):
                            if batch_norm:
                                pe.wait_ge(s_h, n + 1)
                            at_least(pe, s_xh, n - 1)
                            nc.tensor.matmul(cen[par][:, 0:T], centre, Y[:, n, :], start=True, stop=True).then_inc(s_cen, 1)
                        if not (isinstance(n, int) and n == 0):
                            pe.wait_ge(s_rs, n)
                            at_least(pe, s_rb, n - 2)
                            for c in range(NCH):
                                last = nc.tensor.transpose(spr[o][:, c * CH:(c + 1) * CH],
                                                           sd[o][:, NCH + c:NCH + c + 1].broadcast_to([CH, C]), ident[0:CH, 0:CH])
                            last.then_inc(s_spr, 1)
                        if not (isinstance(n, int) and n >= B):
                            pe.wait_ge(s_sq, n + 1)
                            at_least(pe, s_sd, n - 1)
                            for c in range(NCH):
                                last = nc.tensor.matmul(var[par][0:CH, c:c + 1], sq[par][:, c * CH:(c + 1) * CH], mean_m[:, 0:1],
                                                        start=True, stop=True)
                            last.then_inc(s_var, 1)

                    rounds(pe, seq, B, 1)

                @block.scalar
                def _(act):
                    def seq(n, par):
                        o = 1 - par
                        if not (isinstance(n, int) and n == 0):
                            act.wait_ge(s_var, n)
                            at_least(act, s_rs, n - 2)
                            nc.scalar.activation(sd[o][:, 0:NCH], var[o][0:CH, 0:NCH], ACT.Sqrt, bias=eps[0:CH, 0:1]).then_inc(s_sd, 1)
                        if not (isinstance(n, int) and n >= B):
                            act.wait_ge(s_cen, n + 1)
                            at_least(act, s_var, n - 1)
                            nc.scalar.activation(sq[par][:, :], cen[par][:, 0:T], ACT.Square).then_inc(s_sq, 1)
                        if not (isinstance(n, int) and n == 0):
                            act.wait_ge(s_spr, n)
                            at_least(act, s_xh, n - 2)
                            nc.scalar.activation(rb[o][:, :], spr[o][:, 0:T], ACT.Copy).then_inc(s_rb, 1)

                    rounds(act, seq, B, 1)

                @block.vector
                def _(dve):
                    def apply_bn(n):
                        nc.vector.tensor_scalar(Y[:, n, :], Y[:, n, :], bn[:, 2:3], bn[:, 3:4], ALU.mult, ALU.add).then_inc(s_h, 1)

                    def seq(n, par):
                        o = 1 - par
                        if not (isinstance(n, int) and n == 0):
                            dve.wait_ge(s_sd, n)
                            at_least(dve, s_spr, n - 2)
                            nc.vector.reciprocal(sd[o][:, NCH:2 * NCH], sd[o][:, 0:NCH]).then_inc(s_rs, 1)
                        if batch_norm and not (isinstance(n, int) and n >= B):
                            apply_bn(n)
                        if not (isinstance(n, int) and n == 0):
                            dve.wait_ge(s_rb, n)
                            dve.wait_ge(s_cen, n)
                            nc.vector.tensor_tensor(XH[:, n - 1, :], cen[o][:, 0:T], rb[o][:, :], ALU.mult).then_inc(s_xh, 1)

                    rounds(dve, seq, B, 1)

        layer_norm("ln1_", True)

        with ExitStack() as p:
            pq = [[ps(f"proj{j}{i}", on=p) for i in range(2)] for j in range(3)]
            vtp = [ps(f"vt_ps{i}", on=p) for i in range(2)]
            qs = [[sb(f"qkv{j}{i}", [C, T], on=p) for i in range(2)] for j in range(3)]
            vt = [sb(f"vt{i}", [CH, NCH * C], on=p) for i in range(2)]
            s_pr = [sem(f"proj_ready{j}") for j in range(3)]
            s_ge = [sem(f"gelu_ready{j}") for j in range(3)]
            s_vt, s_vc = sem("v_transposed"), sem("v_copied")
            s_store = [sem(f"qkv_stored{i}") for i in range(2)]
            block = p.enter_context(nc.Block())

            def stored(n):
                return 48 * (n // 2)

            @block.tensor
            def _(pe):
                def seq(n, par):
                    o = 1 - par
                    live = not (isinstance(n, int) and n >= B)
                    for j in (0, 1, None, 2):
                        if j is None:
                            if not (isinstance(n, int) and n == 0):
                                pe.wait_ge(s_ge[2], n)
                                at_least(pe, s_vc, n - 2)
                                for c in range(NCH):
                                    last = nc.tensor.transpose(vtp[o][0:CH, c * C:(c + 1) * C], qs[2][o][:, c * CH:(c + 1) * CH], ident)
                                last.then_inc(s_vt, 1)
                        elif live:
                            at_least(pe, s_ge[j], n - 1)
                            nc.tensor.matmul(pq[j][par][:, 0:T], aw[:, j, :], XH[:, n, :], start=True, stop=True).then_inc(s_pr[j], 1)

                rounds(pe, seq, B, 1)

            @block.scalar
            def _(act):
                nc.scalar.preload_act_table(ACT.Gelu)

                def seq(n, par):
                    if not (isinstance(n, int) and n < 2):
                        act.wait_ge(s_store[par], stored(n))
                        act.wait_ge(s_vt, n - 1)
                    for j in range(3):
                        act.wait_ge(s_pr[j], n + 1)
                        nc.scalar.activation(qs[j][par][:, :], pq[j][par][:, 0:T], ACT.Gelu, bias=ab[:, j:j + 1]).then_inc(s_ge[j], 1)

                rounds(act, seq, B)

            @block.vector
            def _(dve):
                def seq(n, par):
                    dve.wait_ge(s_vt, n + 1)
                    if not (isinstance(n, int) and n < 2):
                        dve.wait_ge(s_store[par], stored(n))
                    nc.vector.tensor_copy(vt[par][:, :], vtp[par][0:CH, :]).then_inc(s_vc, 1)

                rounds(dve, seq, B)

            @block.sync
            def _(sp):
                def seq(n, par):
                    sp.wait_ge(s_par, 80)
                    sp.wait_ge(s_ge[0], n + 1)
                    sp.dma_start(q_d[n], qs[0][par][:, :]).then_inc(s_store[par], 16)
                    sp.wait_ge(s_par, 80)
                    sp.wait_ge(s_ge[1], n + 1)
                    sp.dma_start(k_d[n], qs[1][par][:, :]).then_inc(s_store[par], 16)
                    sp.wait_ge(s_par, 80)
                    sp.wait_ge(s_vc, n + 1)
                    sp.dma_start(v_d[n], vt[par][:, :]).then_inc(s_store[par], 16)

                rounds(sp, seq, B)
                sp.wait_ge(s_store[0], 24 * B)
                sp.wait_ge(s_store[1], 24 * B)

        with ExitStack() as p:
            qr = [sb(f"qr{i}", [C, T], on=p) for i in range(2)]
            kr = [sb(f"kr{i}", [C, T], on=p) for i in range(2)]
            vr = [sb(f"vr{i}", [CH, NCH * C], on=p) for i in range(2)]
            qm = [[sb(f"qm{i}{j}", [C, T], on=p) for j in range(2)] for i in range(2)]
            vm = [[sb(f"vm{i}{j}", [CH, NCH * C], on=p) for j in range(2)] for i in range(2)]
            vmk = sb("vmk", [CH, 2, NCH * C], on=p)
            pr = [sb(f"pr{i}", [CH, T], on=p) for i in range(3)]
            pt = [sb(f"pt{i}", [CH, T], on=p) for i in range(8)]
            nm = sb("nm", [CH, 8], on=p)
            rs = [sb(f"rs{i}", [CH, HEADS], on=p) for i in range(2)]
            ri = [sb(f"ri{i}", [CH, HEADS], on=p) for i in range(2)]
            rw = [sb(f"rw{i}", [CH, C], on=p) for i in range(2)]
            ones = sb("ones", [CH, C], on=p)
            rc = sb("rc", [C, CH], on=p)
            s_bank = [ps(f"s{i}", on=p) for i in range(3)]
            t_bank = [ps(f"t{i}", on=p) for i in range(2)]
            o_bank = [ps(f"o{i}", on=p) for i in range(2)]
            r_bank = ps("r", on=p)
            s_mk = sem("masks_loaded")
            s_ld = [sem(f"qkv_loaded{i}") for i in range(2)]
            s_mq, s_s, s_max, s_exp, s_t = sem("qv_masked"), sem("scores_ready"), sem("max_ready"), sem("exp_ready"), sem("p_transposed")
            s_ed, s_ea, s_av = sem("pt_copied_dve"), sem("pt_copied_act"), sem("av_done")
            s_rw, s_ones = sem("rinv_widened"), sem("ones_set")
            s_ri, s_r, s_rc, s_o = sem("rsum_inverted"), sem("rinv_spread"), sem("rinv_in_sbuf"), sem("o_ready")
            block = p.enter_context(nc.Block())
            NH = NCH * HEADS
            QUADS = NH // 4

            @block.sync
            def _(sp):
                sp.dma_start(vmk[:, :, :], vmask).then_inc(s_mk, 16)

                def seq(n, par):
                    if not (isinstance(n, int) and n < 2):
                        sp.wait_ge(s_par, 80)
                        sp.wait_ge(s_av, (n - 1) * QUADS)
                    sp.dma_start(qr[par][:, :], q_d[n]).then_inc(s_ld[par], 16)
                    sp.dma_start(kr[par][:, :], k_d[n]).then_inc(s_ld[par], 16)
                    sp.dma_start(vr[par][:, :], v_d[n]).then_inc(s_ld[par], 16)

                rounds(sp, seq, B)

            @block.gpsimd
            def _(pool):

                nc.gpsimd.memset(ones[:, :], 1.0).then_inc(s_ones, 1)
                pool.wait_ge(s_ones, 1)

                def mask(n, par):
                    pool.wait_ge(s_mk, 16)
                    pool.wait_ge(s_ld[par], 48 * (n // 2 + 1))
                    if not (isinstance(n, int) and n < 2):
                        pool.wait_ge(s_av, (n - 1) * QUADS)
                    for j in range(2):
                        nc.gpsimd.tensor_tensor(qm[par][j][:, :], qr[par][:, :], par_m[:, j:j + 1].broadcast_to([C, T]), ALU.mult).then_inc(s_mq, 1)
                    for j in range(2):
                        nc.gpsimd.tensor_tensor(vm[par][j][:, :], vr[par][:, :], vmk[:, j, :], ALU.mult).then_inc(s_mq, 1)

                def seq(n, par):
                    for c in range(NCH):
                        u = n * NCH + c
                        pool.wait_ge(s_mk, 16)
                        pool.wait_ge(s_ri, u + 1)
                        at_least(pool, s_r, u - 1)
                        wide = ri[c % 2][:, :].rearrange("p (h o) -> p h o", o=1).broadcast_to([CH, HEADS, HD])
                        nc.gpsimd.tensor_tensor(rw[c % 2][:, :].rearrange("p (h d) -> p h d", d=HD), wide,
                                                ones[:, :].rearrange("p (h d) -> p h d", d=HD), ALU.mult).then_inc(s_rw, 1)
                        if c == 0 and not (isinstance(n, int) and n == B - 1):
                            mask(n + 1, 1 - par)

                mask(0, 0)
                seq(0, 0)
                seq(1, 1)
                with pool.Fori(1, B // 2 - 1) as n:
                    seq(2 * n, 0)
                    seq(2 * n + 1, 1)
                seq(B - 2, 0)
                seq(B - 1, 1)

            def place(i):
                return i // HEADS, i // 4 % 2, i % 4

            @block.tensor
            def _(pe):
                def scores(n, i, par):
                    c, j, quad = place(i)
                    g = n * NH + i
                    if i == 0:
                        pe.wait_ge(s_ld[par], 48 * (n // 2 + 1))
                        pe.wait_ge(s_mq, 4 * n + 4)
                    at_least(pe, s_exp, g - 1)
                    rows = slice(32 * quad, 32 * quad + 32)
                    nc.tensor.matmul(s_bank[i % 2][0:CH, 0:T], qm[par][j][rows, c * CH:(c + 1) * CH], kr[par][rows, :],
                                     start=True, stop=True).then_inc(s_s, 1)

                def seq(n, par):
                    for i in range(NH):
                        c, j, quad = place(i)
                        g, u = n * NH + i, n * NCH + c
                        if i + 1 < NH:
                            scores(n, i + 1, par)
                        elif not (isinstance(n, int) and n == B - 1):
                            scores(n + 1, 0, 1 - par)
                        pe.wait_ge(s_exp, g + 1)
                        h2 = n * (NH // 2) + i // 2
                        at_least(pe, s_ea if i % 2 else s_ed, h2)
                        for k in range(NCH):
                            last = nc.tensor.transpose(t_bank[i % 2][0:CH, k * CH:(k + 1) * CH], pr[i % 2][:, k * CH:(k + 1) * CH],
                                                       ident[0:CH, 0:CH])
                        last.then_inc(s_t, 1)
                        if quad == 3:
                            pe.wait_ge(s_ed, h2 + 1)
                            pe.wait_ge(s_ea, h2 + 1)
                            if j == 0:
                                at_least(pe, s_o, u - 1)
                            for k in range(NCH):
                                for q in range(4):
                                    last = nc.tensor.matmul(o_bank[c % 2][32 * q:32 * q + 32, 0:CH],
                                                            vm[par][j][:, k * C + 32 * q:k * C + 32 * q + 32],
                                                            pt[4 * j + q][:, k * CH:(k + 1) * CH],
                                                            start=j == 0 and k == 0, stop=j == 1 and k == NCH - 1)
                            last.then_inc(s_av, 1)
                            if j == 1:
                                pe.wait_ge(s_rw, u + 1)
                                at_least(pe, s_rc, u)
                                nc.tensor.transpose(r_bank[:, 0:CH], rw[c % 2][:, :], ident[0:CH, 0:CH]).then_inc(s_r, 1)

                scores(0, 0, 0)
                seq(0, 0)
                seq(1, 1)
                with pe.Fori(1, B // 2 - 1) as n:
                    seq(2 * n, 0)
                    seq(2 * n + 1, 1)
                seq(B - 2, 0)
                seq(B - 1, 1)

            @block.scalar
            def _(act):
                nc.scalar.preload_act_table(ACT.Exp)

                def copy_pt(n, i):
                    g = n * NH + i
                    act.wait_ge(s_t, g + 1)
                    at_least(act, s_av, n * QUADS + i // 4 - 1)
                    nc.scalar.activation(pt[i % 8][:, :], t_bank[i % 2][0:CH, 0:T], ACT.Copy).then_inc(s_ea, 1)

                def copy_rc(u):
                    act.wait_ge(s_r, u + 1)
                    at_least(act, s_o, u)
                    nc.scalar.activation(rc[:, :], r_bank[:, 0:CH], ACT.Copy).then_inc(s_rc, 1)

                def seq(n, par):
                    for i in range(NH):
                        c, j, quad = place(i)
                        g, u = n * NH + i, n * NCH + c
                        act.wait_ge(s_max, g + 1)
                        at_least(act, s_t, g - 1)
                        if i % HEADS == 0:
                            at_least(act, s_ri, u - 1)
                        nc.scalar.activation(pr[i % 2][:, :], s_bank[i % 2][0:CH, 0:T], ACT.Exp, bias=nm[:, i % 8:i % 8 + 1],
                                             accum_out=rs[c % 2][:, i % 8:i % 8 + 1]).then_inc(s_exp, 1)
                        if i % 2 == 0 and not (isinstance(n, int) and g == 0):
                            copy_pt(n - 1 if i == 0 else n, (i - 1) % NH)
                        if i % HEADS == 2 and not (isinstance(n, int) and u == 0):
                            copy_rc(u - 1)

                rounds(act, seq, B)
                copy_pt(B - 1, NH - 1)
                copy_rc(B * NCH - 1)

            @block.vector
            def _(dve):
                def row_max(n, i):
                    g = n * NH + i
                    dve.wait_ge(s_s, g + 1)
                    at_least(dve, s_exp, g - 7)
                    nc.vector.tensor_reduce(nm[:, i % 8:i % 8 + 1], s_bank[i % 2][0:CH, 0:T], AX, ALU.max, negate=True).then_inc(s_max, 1)

                def finish(n, c):
                    u = n * NCH + c
                    dve.wait_ge(s_rc, u + 1)
                    dve.wait_ge(s_av, 2 * u + 2)
                    nc.vector.tensor_tensor(XH[:, n, c * CH:(c + 1) * CH], o_bank[c % 2][:, 0:CH], rc[:, :], ALU.mult).then_inc(s_o, 1)

                def seq(n, par):
                    for i in range(NH):
                        c, j, quad = place(i)
                        g, u = n * NH + i, n * NCH + c
                        if i + 1 < NH:
                            row_max(n, i + 1)
                        elif not (isinstance(n, int) and n == B - 1):
                            row_max(n + 1, 0)
                        if i % 2 == 0:
                            dve.wait_ge(s_t, g + 1)
                            at_least(dve, s_av, n * QUADS + i // 4 - 1)
                            nc.vector.tensor_copy(pt[i % 8][:, :], t_bank[0][0:CH, 0:T]).then_inc(s_ed, 1)
                        if i % HEADS == HEADS - 1:
                            dve.wait_ge(s_exp, g + 1)
                            at_least(dve, s_rw, u - 1)
                            nc.vector.reciprocal(ri[c % 2][:, :].rearrange("p (q j) -> p j q", j=2),
                                                 rs[c % 2][:, :].rearrange("p (j q) -> p j q", j=2)).then_inc(s_ri, 1)
                        if i % HEADS == 4 and not (isinstance(n, int) and u == 0):
                            finish(n - 1 if c == 0 else n, (c - 1) % NCH)

                row_max(0, 0)
                seq(0, 0)
                seq(1, 1)
                with dve.Fori(1, B // 2 - 1) as n:
                    seq(2 * n, 0)
                    seq(2 * n + 1, 1)
                seq(B - 2, 0)
                seq(B - 1, 1)
                finish(B - 1, NCH - 1)

        with ExitStack() as p:
            wps = [ps(f"wo_ps{i}", on=p) for i in range(2)]
            gb = [sb(f"gb{i}", [C, T], on=p) for i in range(2)]
            s_wo, s_go, s_add = sem("wo_ready"), sem("wo_gelu"), sem("residual_added")
            block = p.enter_context(nc.Block())

            @block.tensor
            def _(pe):
                def seq(n, par):
                    at_least(pe, s_go, n - 1)
                    nc.tensor.matmul(wps[par][:, 0:T], aw[:, 3, :], XH[:, n, :], start=True, stop=True).then_inc(s_wo, 1)

                rounds(pe, seq, B)

            @block.scalar
            def _(act):
                nc.scalar.preload_act_table(ACT.Gelu)

                def seq(n, par):
                    act.wait_ge(s_wo, n + 1)
                    at_least(act, s_add, n - 1)
                    nc.scalar.activation(gb[par][:, :], wps[par][:, 0:T], ACT.Gelu, bias=ab[:, 3:4]).then_inc(s_go, 1)

                rounds(act, seq, B)

            @block.vector
            def _(dve):
                def seq(n, par):
                    dve.wait_ge(s_go, n + 1)
                    nc.vector.tensor_tensor(Y[:, n, :], Y[:, n, :], gb[par][:, :], ALU.add).then_inc(s_add, 1)

                rounds(dve, seq, B)

        layer_norm("ln2_", False)

        with ExitStack() as p:
            FI, G, LO, W_ALL = slice(0, 2 * C), slice(2 * C, 3 * C), slice(3 * C, 4 * C + S), 4 * C + S
            L, O = slice(0, S), slice(S, S + C)
            wx, wh = sb("wx", [C, S, W_ALL], on=p), sb("wh", [C, S, W_ALL], on=p)
            wc = sb("wc", [C, S], on=p)
            rows = 3 * S
            bi, bh = sb("bi", [rows, W_ALL], on=p), sb("bh", [rows, W_ALL], on=p)
            bsplit = [sb(f"bsplit{i}", [rows, W_ALL], bf16, on=p) for i in range(3)]
            bw = sb("bw", [rows, W_ALL], bf16, on=p)
            ind = sb("ind", [rows, C], bf16, on=p)
            xs = sb("xs", [C, STEPS, B], on=p)
            hs = sb("hs", [C, STEPS, 2, B], on=p)
            ob = [sb(f"ob{i}", [C, 4, B], on=p) for i in range(4)]
            fi = [sb(f"fi{i}", [C, 2 * C], on=p) for i in range(2)]
            tg = [sb(f"tg{i}", [C, C], on=p) for i in range(2)]
            to = [sb(f"to{i}", [C, C], on=p) for i in range(2)]
            tc = [sb(f"tc{i}", [C, C], on=p) for i in range(2)]
            uu, vv = sb("uu", [C, C], on=p), sb("vv", [C, C], on=p)
            c2 = [sb(f"c2{i}", [C, C], on=p) for i in range(2)]
            h2 = [sb(f"h2{i}", [C, C], on=p) for i in range(2)]
            lg = [sb(f"lg{i}", [C, S], on=p) for i in range(2)]
            lm, lq, le = sb("lm", [C, 1], on=p), sb("lq", [C, 1], on=p), sb("le", [C, S], on=p)
            sel = [sb(f"sel{i}", [C, C], on=p) for i in range(2)]
            zero = sb("zero", [C, B], on=p)
            g_fi, g_g, g_lo = ps("g_fi", on=p), ps("g_g", on=p), ps("g_lo", on=p)
            hc, cr = ps("hc", on=p), ps("cr", on=p)
            s_w, s_sc, s_bz = sem("lstm_loaded"), sem("lstm_scaled"), sem("bias_chain")
            s_z = sem("state_zeroed")
            s_xs, s_xu = sem("x_staged"), sem("x_used")
            s_fi, s_g, s_lo = sem("fi_ready"), sem("g_ready"), sem("logits_o_ready")
            s_tfi, s_tg, s_lg, s_to, s_tc = sem("fi_tanh"), sem("g_tanh"), sem("logits_in_sbuf"), sem("o_tanh"), sem("c_tanh")
            s_m, s_q, s_sel = sem("logit_max"), sem("chosen"), sem("sel_ready")
            s_u, s_v, s_c2, s_h2 = sem("u_ready"), sem("v_ready"), sem("c2_ready"), sem("h2_ready")
            s_crep, s_htp, s_htc = sem("crep_ready"), sem("state_ready"), sem("state_copied")
            s_ob, s_out = sem("out_ready"), [sem(f"out_stored{i}") for i in range(4)]
            block = p.enter_context(nc.Block())
            NB = T // STEPS
            QS = STEPS // 4
            LOADS = 3 + 2 * 3

            @block.sync
            def _(sp):
                sp.dma_start(wx[:, :, :], w_ih).then_inc(s_w, 16)
                sp.dma_start(wh[:, :, :], w_hh).then_inc(s_w, 16)
                sp.dma_start(wc[:, :], w_selc).then_inc(s_w, 16)
                for k in range(3):
                    sp.dma_start(bi[k * S:(k + 1) * S, :], b_ih).then_inc(s_w, 16)
                    sp.dma_start(bh[k * S:(k + 1) * S, :], b_hh).then_inc(s_w, 16)

                def body(it):
                    for q in range(QS):
                        sp.wait_ge(s_par, 80)
                        sp.wait_ge(s_ob, it * QS + q + 1)
                        sp.dma_start(out[:, bass.ds(it * STEPS + 4 * q, 4), :], ob[q][:, :, :]).then_inc(s_out[q], 16)

                body(0)
                with sp.Fori(1, NB) as it:
                    body(it)
                for q in range(QS):
                    sp.wait_ge(s_out[q], 16 * NB)

            @block.gpsimd
            def _(pool):
                def stage(it, q, first):
                    pool.wait_ge(s_par, 80)
                    if not first:
                        pool.wait_ge(s_xu, (it - 1) * STEPS + 4 * q + 4)
                    nc.gpsimd.tensor_copy(xs[:, 4 * q:4 * q + 4, :],
                                          XH[:, :, bass.ds(it * STEPS + 4 * q, 4)].rearrange("p b t -> p t b")).then_inc(s_xs, 1)

                def body(it, first, last):
                    for q in range(QS):
                        if not last:
                            stage(it + 1, q, False)
                        pool.wait_ge(s_htc, it * STEPS + 4 * q + 4)
                        if not first:
                            pool.wait_ge(s_out[q], it * 16)
                        nc.gpsimd.tensor_tensor(ob[q][:, :, :], hs[:, 4 * q:4 * q + 4, 1, :],
                                                Y[:, :, bass.ds(it * STEPS + 4 * q, 4)].rearrange("p b t -> p t b"),
                                                ALU.add).then_inc(s_ob, 1)

                for q in range(QS):
                    stage(0, q, True)
                body(0, True, False)
                with pool.Fori(1, NB - 1) as it:
                    body(it, False, False)
                body(NB - 1, False, True)

            @block.tensor
            def _(pe):
                def x_part(bank, cols, k):
                    n = cols.stop - cols.start
                    for s in range(S):
                        nc.tensor.matmul(bank[32 * s:32 * s + 32, 0:n], xs[:, k, :], wx[:, s, cols],
                                         start=True, stop=False, skip_group_check=True)
                    return nc.tensor.matmul(bank[:, 0:n], ind[:, :], bw[:, cols], start=False, stop=False, skip_group_check=True)

                def state_part(bank, state, w, cols, stop=True):
                    n = cols.stop - cols.start
                    for s in range(S):
                        last = nc.tensor.matmul(bank[32 * s:32 * s + 32, 0:n], state, w[:, s, cols] if w is wh else w,
                                                start=False, stop=stop, skip_group_check=True)
                    return last

                def step(it, k, first, last):
                    t = it * STEPS + k
                    par = k % 2
                    hk = zero[:, :] if first else hs[:, (k - 1) % STEPS, 1, :]
                    ck = zero[:, :] if first else hs[:, (k - 1) % STEPS, 0, :]
                    if not first:
                        pe.wait_ge(s_htc, t)
                    state_part(g_fi, hk, wh, FI).then_inc(s_fi, 1)
                    state_part(g_g, hk, wh, G).then_inc(s_g, 1)
                    state_part(g_lo, ck, wc[:, :], L, False)
                    state_part(g_lo, hk, wh, LO).then_inc(s_lo, 1)
                    nk = (k + 1) % STEPS
                    if not last:
                        if nk % 4 == 0:
                            pe.wait_ge(s_xs, it * QS + (k + 1) // 4 + 1)
                        pe.wait_ge(s_tfi, t + 1)
                        x_part(g_fi, FI, nk)
                        pe.wait_ge(s_tg, t + 1)
                        x_part(g_g, G, nk)
                    pe.wait_ge(s_sel, t + 1)
                    pe.wait_ge(s_c2, t + 1)
                    nc.tensor.matmul(hc[:, 0:B], c2[par][:, :], sel[par][:, 0:B], start=True, stop=True)
                    pe.wait_ge(s_h2, t + 1)
                    nc.tensor.matmul(hc[:, B:2 * B], h2[par][:, :], sel[par][:, 0:B], start=True, stop=True).then_inc(s_htp, 1)
                    if not last:
                        nc.tensor.matmul(cr[:, 0:C], sel[par][:, :], c2[par][:, :], start=True, stop=True).then_inc(s_crep, 1)
                        pe.wait_ge(s_to, t + 1)
                        x_part(g_lo, LO, nk).then_inc(s_xu, 1)

                def body(it, first, last):
                    for k in range(STEPS):
                        step(it, k, first and k == 0, last and k == STEPS - 1)

                pe.wait_ge(s_w, 16 * LOADS)
                pe.wait_ge(s_sc, 4)
                pe.wait_ge(s_z, 1)
                pe.wait_ge(s_xs, 1)
                x_part(g_fi, FI, 0)
                x_part(g_g, G, 0)
                x_part(g_lo, LO, 0).then_inc(s_xu, 1)
                body(0, True, False)
                with pe.Fori(1, NB - 1) as it:
                    body(it, False, False)
                body(NB - 1, False, True)

            @block.scalar
            def _(act):
                nc.scalar.preload_act_table(ACT.Tanh)

                def step(t, k):
                    par = k % 2
                    act.wait_ge(s_fi, t + 1)
                    at_least(act, s_u, t - 1)
                    nc.scalar.activation(fi[par][:, :], g_fi[:, 0:2 * C], ACT.Tanh).then_inc(s_tfi, 1)
                    act.wait_ge(s_g, t + 1)
                    nc.scalar.activation(tg[par][:, :], g_g[:, 0:C], ACT.Tanh).then_inc(s_tg, 1)
                    act.wait_ge(s_lo, t + 1)
                    at_least(act, s_q, t - 2)
                    nc.scalar.activation(lg[par][:, :], g_lo[:, L], ACT.Copy).then_inc(s_lg, 1)
                    at_least(act, s_h2, t - 1)
                    nc.scalar.activation(to[par][:, :], g_lo[:, O], ACT.Tanh).then_inc(s_to, 1)
                    act.wait_ge(s_c2, t + 1)
                    nc.scalar.activation(tc[par][:, :], c2[par][:, :], ACT.Tanh, scale=0.5).then_inc(s_tc, 1)

                def body(it):
                    for k in range(STEPS):
                        step(it * STEPS + k, k)

                body(0)
                with act.Fori(1, NB) as it:
                    body(it)

            @block.vector
            def _(dve):
                nc.vector.memset(zero[:, :], 0.0).then_inc(s_z, 1)
                dve.wait_ge(s_w, 16 * LOADS)
                OG = slice(3 * C + S, 4 * C + S)
                for w in (wx, wh):
                    nc.vector.tensor_scalar(w[:, :, FI], w[:, :, FI], 0.5, None, ALU.mult).then_inc(s_bz, 1)
                    nc.vector.tensor_scalar(w[:, :, OG], w[:, :, OG], 0.5, None, ALU.mult).then_inc(s_bz, 1)
                nc.vector.tensor_copy(ind[:, :], kc[0:rows, COLS[K_IND]:COLS[K_IND] + C]).then_inc(s_bz, 1)
                nc.vector.tensor_tensor(bi[:, :], bi[:, :], bh[:, :], ALU.add).then_inc(s_bz, 1)
                dve.wait_ge(s_bz, 6)
                nc.vector.tensor_scalar(bi[:, FI], bi[:, FI], 0.5, None, ALU.mult).then_inc(s_bz, 1)
                nc.vector.tensor_scalar(bi[:, OG], bi[:, OG], 0.5, None, ALU.mult).then_inc(s_bz, 1)
                dve.wait_ge(s_bz, 8)
                nc.vector.tensor_copy(bsplit[0][:, :], bi[:, :]).then_inc(s_bz, 1)
                dve.wait_ge(s_bz, 9)
                nc.vector.tensor_tensor(bi[:, :], bi[:, :], bsplit[0][:, :], ALU.subtract).then_inc(s_bz, 1)
                dve.wait_ge(s_bz, 10)
                nc.vector.tensor_copy(bsplit[1][:, :], bi[:, :]).then_inc(s_bz, 1)
                dve.wait_ge(s_bz, 11)
                nc.vector.tensor_tensor(bi[:, :], bi[:, :], bsplit[1][:, :], ALU.subtract).then_inc(s_bz, 1)
                dve.wait_ge(s_bz, 12)
                nc.vector.tensor_copy(bsplit[2][:, :], bi[:, :]).then_inc(s_bz, 1)
                part = kc[0:rows, COLS[K_PART]:COLS[K_PART] + 3]
                nc.vector.tensor_scalar(bw[:, :], bsplit[0][:, :], part[:, 0:1], None, ALU.mult).then_inc(s_bz, 1)
                dve.wait_ge(s_bz, 14)
                for k in (1, 2):
                    nc.vector.scalar_tensor_tensor(bw[:, :], bsplit[k][:, :], part[:, k:k + 1], bw[:, :], ALU.mult, ALU.add).then_inc(s_bz, 1)
                    dve.wait_ge(s_bz, 14 + k)
                nc.vector.engine_nop().then_inc(s_sc, 4)

                def step(it, k, first, early):
                    t = it * STEPS + k
                    par = k % 2
                    dve.wait_ge(s_tfi, t + 1)
                    if first:
                        nc.vector.memset(vv[:, :], 0.0).then_inc(s_v, 1)
                        dve.wait_ge(s_v, 1)
                    else:
                        dve.wait_ge(s_crep, t)
                        nc.vector.scalar_tensor_tensor(vv[:, :], fi[par][:, 0:C], 1.0, cr[:, 0:C], ALU.add, ALU.mult).then_inc(s_v, 1)
                    dve.wait_ge(s_tg, t + 1)
                    nc.vector.scalar_tensor_tensor(uu[:, :], fi[par][:, C:2 * C], 1.0, tg[par][:, :], ALU.add, ALU.mult).then_inc(s_u, 1)
                    dve.wait_ge(s_lg, t + 1)
                    if not first:
                        nc.vector.tensor_reduce(lm[:, :], lg[par][:, :], AX, ALU.max).then_inc(s_m, 1)
                    dve.wait_ge(s_u, t + 1)
                    nc.vector.tensor_tensor(c2[par][:, :], uu[:, :], vv[:, :], ALU.add).then_inc(s_c2, 1)
                    if first:
                        nc.vector.tensor_copy(sel[par][:, :], const(K_SEL0)).then_inc(s_sel, 1)
                    else:
                        dve.wait_ge(s_m, t)
                        nc.vector.scalar_tensor_tensor(le[:, :], lg[par][:, :], lm[:, 0:1], first_w, ALU.is_ge, ALU.mult,
                                                       accum_out=lq[:, :]).then_inc(s_q, 1)
                        dve.wait_ge(s_q, t)
                        nc.vector.tensor_scalar(sel[par][:, :], pick, lq[:, 0:1], 0.0, ALU.mult, ALU.max).then_inc(s_sel, 1)
                    dve.wait_ge(s_to, t + 1)
                    dve.wait_ge(s_tc, t + 1)
                    nc.vector.scalar_tensor_tensor(h2[par][:, :], to[par][:, :], 1.0, tc[par][:, :], ALU.add, ALU.mult).then_inc(s_h2, 1)
                    dve.wait_ge(s_htp, t + 1)
                    if k % 4 == 0 and not early:
                        dve.wait_ge(s_ob, it * QS + k // 4 - QS + 1)
                    nc.vector.tensor_copy(hs[:, k, :, :], hc[:, 0:2 * B].rearrange("p (a b) -> p a b", a=2)).then_inc(s_htc, 1)

                def body(it, early):
                    for k in range(STEPS):
                        step(it, k, early and k == 0, early)

                body(0, True)
                with dve.Fori(1, NB) as it:
                    body(it, False)


def constants():
    import numpy as np
    k = np.zeros((128, COLS[-1]), np.float32)
    p = np.arange(128)

    def put(which, a):
        k[:a.shape[0], COLS[which]:COLS[which] + a.shape[1]] = a

    same = (p[:, None] % 32 == p[None, :] % 32).astype(np.float32)
    put(K_ID, np.eye(128, dtype=np.float32))
    put(K_PICK, 0.5 * same)
    put(K_CENTRE, np.eye(128, dtype=np.float32) - np.float32(1 / 128))
    put(K_MEAN, np.full((128, 128), 1 / 128, np.float32))
    module, s = p[:, None] // 32, np.arange(S)[None, :]
    put(K_FIRST, np.where(s == module, 1, np.where(s < module, -8, 0)).astype(np.float32))
    put(K_PAR, np.stack([(p // 16 % 2 == j) * 0.25 for j in range(2)], 1).astype(np.float32))
    put(K_IND, (np.arange(3 * S)[:, None] % S == p[None, :] // 32).astype(np.float32))
    put(K_PART, (np.arange(3 * S)[:, None] // S == np.arange(3)[None, :]).astype(np.float32))
    put(K_SEL0, 0.5 * same * (p[:, None] < 32))
    col = np.arange(4 * 128) % 128 // 16 % 2
    vmask = np.broadcast_to(np.stack([col == j for j in range(2)]).astype(np.float32), (CH, 2, 512)).copy()
    return k, vmask


def kernel(**inputs):
    import numpy as np
    import concourse.bacc as bacc
    from concourse.bass_utils import run_bass_kernel_spmd

    a = {k: np.asarray(v) for k, v in inputs.items()}
    gates = [1, 0, 2, 3]

    def lstm_w(w, w_sel):
        g = w.reshape(S, 4, C, C)[:, gates].reshape(S, 4 * C, C)
        sel = np.broadcast_to(w_sel, (S, S, C))
        return np.concatenate([g[:, :3 * C], sel, g[:, 3 * C:]], 1).transpose(2, 0, 1)

    def lstm_b(b, b_sel):
        g = b.reshape(S, 4, C)[:, gates].reshape(S, 4 * C)
        return np.concatenate([g[:, :3 * C], np.broadcast_to(b_sel, (S, S)), g[:, 3 * C:]], 1)

    tok = a["L0_tok_W"].T
    tokw = np.zeros((128, 3, C), np.float32)
    tokw[:, 0], tokw[:, 1], tokw[:D, 2] = tok[0:128], tok[128:256], tok[256:320]
    w_sel = a["L0_ffn_W_sel"].reshape(S, 3, C)
    consts, vmask = constants()
    data = {
        "x": a["x"].transpose(2, 0, 1).reshape(D, B * T_IN),
        "tok_w": tokw,
        "tok_v": np.stack([a["L0_tok_b"], a["L0_tok_gamma"], a["L0_tok_beta"]], 1),
        "attn_w": np.stack([a[f"L0_attn_W{n}"].T for n in "qkvo"], 1),
        "attn_b": np.stack([a[f"L0_attn_b{n}"] for n in "qkvo"], 1),
        "w_ih": lstm_w(a["L0_ffn_W_ih"], w_sel[:, 2]),
        "w_hh": lstm_w(a["L0_ffn_W_hh"], w_sel[:, 0]),
        "w_selc": w_sel[:, 1].T,
        "b_ih": lstm_b(a["L0_ffn_b_ih"], a["L0_ffn_b_sel"]),
        "b_hh": lstm_b(a["L0_ffn_b_hh"], np.zeros(S, np.float32)),
        "consts": consts,
        "vmask": vmask,
    }
    nc = bacc.Bacc("TRN2", target_bir_lowering=False, num_devices=1)
    arrays, args = {}, []
    for name, v in data.items():
        v = np.ascontiguousarray(v)
        arrays[name + "_dram"] = v
        args.append(nc.dram_tensor(name + "_dram", v.shape, mybir.dt.from_np(v.dtype), kind="ExternalInput").ap())
    out = nc.dram_tensor("out_dram", (C, T, B), mybir.dt.float32, kind="ExternalOutput").ap()
    audio_tower(nc, *args, out)
    r = run_bass_kernel_spmd(nc, [arrays], core_ids=[0])
    return np.ascontiguousarray(np.asarray(r.results[0]["out_dram"]).transpose(2, 1, 0))
```

```python
import concourse.bass as bass
from concourse import mybir
from contextlib import ExitStack

B, T_IN, D, TAPS = 32, 500, 64, 5
T = T_IN - TAPS + 1
C = 128
HEADS, HD = 8, 16
CH = 124
NCH = T // CH
S = 4
EPS = 1e-5
STEPS = 16
PIECES = 4
PARTS = 3
PAIRS = [(0, 0), (0, 1), (1, 0), (1, 1), (0, 2), (2, 0)]
KROWS = len(PAIRS) * HD

K_ID, K_PICK, K_CENTRE, K_MEAN, K_FIRST, K_IND, K_PART, K_SEL0 = range(8)
WIDTHS = [C, C, C, C, S, C, 3, C]
COLS = [sum(WIDTHS[:n]) for n in range(len(WIDTHS) + 1)]


def audio_tower(nc, x, tok_w, tok_v, attn_w, attn_b, w_ih, w_hh, w_selc, b_ih, b_hh, consts, out):
    f32, bf16 = mybir.dt.float32, mybir.dt.bfloat16
    ALU, ACT = mybir.AluOpType, mybir.ActivationFunctionType
    AX = mybir.AxisListType.X

    def at_least(eng, sem, n):
        if not (isinstance(n, int) and n <= 0):
            eng.wait_ge(sem, n)

    def rounds(eng, body, total, tail=0):
        body(0, 0)
        body(1, 1)
        with eng.Fori(1, total // 2) as i:
            body(2 * i, 0)
            body(2 * i + 1, 1)
        for n in range(total, total + tail):
            body(n, n % 2)

    stack = ExitStack()
    with stack:
        def sb(name, shape, dt=f32, on=stack):
            return on.enter_context(nc.sbuf_tensor(name, shape, dt))

        def ps(name, on=stack):
            return on.enter_context(nc.psum_tensor(name, [128, 512], f32))

        def sem(name):
            return stack.enter_context(nc.semaphore(name))

        Y = sb("Y", [C, B, T])
        X = sb("X", [C, B * T_IN])
        XH = X[:, 0:B * T].rearrange("p (b t) -> p b t", b=B)
        kc = sb("kc", [128, COLS[-1]])

        def const(k):
            return kc[:, COLS[k]:COLS[k] + WIDTHS[k]]

        ident, pick, centre, mean_m, first_w = (const(k) for k in range(5))
        tokw = sb("tokw", [128, 3, C])
        tokv = sb("tokv", [C, 3])
        bn = sb("bn", [C, 4])
        eps = sb("eps", [128, 1])
        aw = sb("aw", [C, 4, C])
        ab = sb("ab", [C, 4])
        q_d = nc.dram_tensor("q_scratch", [B, C, PARTS, T], bf16, kind="Internal").ap()
        k_d = nc.dram_tensor("k_scratch", [B, C, PARTS, T], bf16, kind="Internal").ap()
        v_d = nc.dram_tensor("v_scratch", [B, CH, NCH, HEADS, 2 * HD], f32, kind="Internal").ap()

        with ExitStack() as p:
            stats = sb("stats", [C, B, 6], on=p)
            mv = sb("mv", [C, 2], on=p)
            cps = [ps(f"conv{i}", on=p) for i in range(2)]
            s_par, s_eps = sem("params_loaded"), sem("eps_set")
            s_x = [sem(f"x_loaded{i}") for i in range(PIECES)]
            s_conv, s_relu, s_st = sem("conv_ready"), sem("relu_ready"), sem("stats_ready")
            s_mv, s_std, s_bn = sem("bn_moments"), sem("bn_std"), sem("bn_chain")
            block = p.enter_context(nc.Block())
            half = B * T_IN // PIECES

            @block.sync
            def _(sp):
                sp.dma_start(tokw[:, :, :], tok_w).then_inc(s_par, 16)
                sp.dma_start(tokv[:, :], tok_v).then_inc(s_par, 16)
                for i in range(PIECES):
                    n = min(half, B * T_IN - 1 - i * half)
                    sp.dma_start(X[0:D, i * half:(i + 1) * half], x[:, i * half:(i + 1) * half]).then_inc(s_x[i], 16)
                    sp.dma_start(X[D:2 * D, i * half:i * half + n], x[:, i * half + 1:i * half + 1 + n]).then_inc(s_x[i], 16)
                sp.dma_start(kc[:, :], consts).then_inc(s_par, 16)
                sp.dma_start(aw[:, :, :], attn_w).then_inc(s_par, 16)
                sp.dma_start(ab[:, :], attn_b).then_inc(s_par, 16)
                sp.wait_ge(s_par, 80)

            @block.tensor
            def _(pe):
                pe.wait_ge(s_par, 80)

                def seq(n, par):
                    at_least(pe, s_relu, n - 1)
                    at = n * T_IN
                    nc.tensor.matmul(cps[par][:, 0:T], tokw[:, 0, :], X[:, bass.ds(at, T)], start=True, stop=False)
                    nc.tensor.matmul(cps[par][:, 0:T], tokw[:, 1, :], X[:, bass.ds(at + 2, T)], start=False, stop=False)
                    nc.tensor.matmul(cps[par][:, 0:T], tokw[0:D, 2, :], X[0:D, bass.ds(at + 4, T)],
                                     start=False, stop=True).then_inc(s_conv, 1)

                each = B // PIECES
                for i in range(PIECES):
                    pe.wait_ge(s_x[i], 32)
                    if i + 1 < PIECES:
                        pe.wait_ge(s_x[i + 1], 32)
                    if i == 0:
                        seq(0, 0)
                        seq(1, 1)
                    with pe.Fori(i * each // 2 + (1 if i == 0 else 0), (i + 1) * each // 2) as n:
                        seq(2 * n, 0)
                        seq(2 * n + 1, 1)

            @block.scalar
            def _(act):
                act.wait_ge(s_par, 80)

                def seq(n, par):
                    act.wait_ge(s_conv, n + 1)
                    nc.scalar.activation(Y[:, n, :], cps[par][:, 0:T], ACT.Relu, bias=tokv[:, 0:1]).then_inc(s_relu, 1)

                rounds(act, seq, B)
                act.wait_ge(s_mv, 1)
                act.wait_ge(s_eps, 1)
                nc.scalar.activation(bn[:, 0:1], mv[:, 1:2], ACT.Sqrt, bias=eps[:, 0:1]).then_inc(s_std, 1)

            @block.vector
            def _(dve):
                nc.vector.memset(eps[:, :], EPS).then_inc(s_eps, 1)

                def seq(n, par):
                    dve.wait_ge(s_relu, n + 1)
                    nc.vector.bn_stats(stats[:, n, :], Y[:, n, :]).then_inc(s_st, 1)

                rounds(dve, seq, B)
                dve.wait_ge(s_st, B)
                nc.vector.bn_aggr(mv[:, :], stats[:, :, :].rearrange("p b s -> p (b s)")).then_inc(s_mv, 1)
                dve.wait_ge(s_std, 1)
                nc.vector.reciprocal(bn[:, 1:2], bn[:, 0:1]).then_inc(s_bn, 1)
                dve.wait_ge(s_bn, 1)
                nc.vector.tensor_tensor(bn[:, 2:3], bn[:, 1:2], tokv[:, 1:2], ALU.mult).then_inc(s_bn, 1)
                dve.wait_ge(s_bn, 2)
                nc.vector.tensor_tensor(bn[:, 3:4], mv[:, 0:1], bn[:, 2:3], ALU.mult).then_inc(s_bn, 1)
                dve.wait_ge(s_bn, 3)
                nc.vector.tensor_tensor(bn[:, 3:4], tokv[:, 2:3], bn[:, 3:4], ALU.subtract).then_inc(s_bn, 1)

        def layer_norm(tag, batch_norm):
            with ExitStack() as p:
                sq = [sb(f"{tag}sq{i}", [C, T], on=p) for i in range(2)]
                rb = [sb(f"{tag}rb{i}", [C, T], on=p) for i in range(2)]
                sd = [sb(f"{tag}sd{i}", [CH, 2 * NCH], on=p) for i in range(2)]
                cen = [ps(f"{tag}cen{i}", on=p) for i in range(2)]
                var = [ps(f"{tag}var{i}", on=p) for i in range(2)]
                spr = [ps(f"{tag}spr{i}", on=p) for i in range(2)]
                s_h, s_cen, s_sq, s_var = (sem(tag + n) for n in ("h_ready", "centred", "squared", "var_ready"))
                s_sd, s_rs, s_spr, s_rb, s_xh = (sem(tag + n) for n in ("std_ready", "rstd_ready", "spread", "rstd_in_sbuf", "xhat_ready"))
                block = p.enter_context(nc.Block())

                @block.tensor
                def _(pe):
                    def seq(n, par):
                        o = 1 - par
                        if not (isinstance(n, int) and n >= B):
                            if batch_norm:
                                pe.wait_ge(s_h, n + 1)
                            at_least(pe, s_xh, n - 1)
                            nc.tensor.matmul(cen[par][:, 0:T], centre, Y[:, n, :], start=True, stop=True).then_inc(s_cen, 1)
                        if not (isinstance(n, int) and n == 0):
                            pe.wait_ge(s_rs, n)
                            at_least(pe, s_rb, n - 2)
                            for c in range(NCH):
                                last = nc.tensor.transpose(spr[o][:, c * CH:(c + 1) * CH],
                                                           sd[o][:, NCH + c:NCH + c + 1].broadcast_to([CH, C]), ident[0:CH, 0:CH])
                            last.then_inc(s_spr, 1)
                        if not (isinstance(n, int) and n >= B):
                            pe.wait_ge(s_sq, n + 1)
                            at_least(pe, s_sd, n - 1)
                            for c in range(NCH):
                                last = nc.tensor.matmul(var[par][0:CH, c:c + 1], sq[par][:, c * CH:(c + 1) * CH], mean_m[:, 0:1],
                                                        start=True, stop=True)
                            last.then_inc(s_var, 1)

                    rounds(pe, seq, B, 1)

                @block.scalar
                def _(act):
                    def seq(n, par):
                        o = 1 - par
                        if not (isinstance(n, int) and n == 0):
                            act.wait_ge(s_var, n)
                            at_least(act, s_rs, n - 2)
                            nc.scalar.activation(sd[o][:, 0:NCH], var[o][0:CH, 0:NCH], ACT.Sqrt, bias=eps[0:CH, 0:1]).then_inc(s_sd, 1)
                        if not (isinstance(n, int) and n >= B):
                            act.wait_ge(s_cen, n + 1)
                            at_least(act, s_var, n - 1)
                            nc.scalar.activation(sq[par][:, :], cen[par][:, 0:T], ACT.Square).then_inc(s_sq, 1)
                        if not (isinstance(n, int) and n == 0):
                            act.wait_ge(s_spr, n)
                            at_least(act, s_xh, n - 2)
                            nc.scalar.activation(rb[o][:, :], spr[o][:, 0:T], ACT.Copy).then_inc(s_rb, 1)

                    rounds(act, seq, B, 1)

                @block.vector
                def _(dve):
                    def apply_bn(n):
                        nc.vector.tensor_scalar(Y[:, n, :], Y[:, n, :], bn[:, 2:3], bn[:, 3:4], ALU.mult, ALU.add).then_inc(s_h, 1)

                    def seq(n, par):
                        o = 1 - par
                        if not (isinstance(n, int) and n == 0):
                            dve.wait_ge(s_sd, n)
                            at_least(dve, s_spr, n - 2)
                            nc.vector.reciprocal(sd[o][:, NCH:2 * NCH], sd[o][:, 0:NCH]).then_inc(s_rs, 1)
                        if batch_norm and not (isinstance(n, int) and n >= B):
                            apply_bn(n)
                        if not (isinstance(n, int) and n == 0):
                            dve.wait_ge(s_rb, n)
                            dve.wait_ge(s_cen, n)
                            nc.vector.tensor_tensor(XH[:, n - 1, :], cen[o][:, 0:T], rb[o][:, :], ALU.mult).then_inc(s_xh, 1)

                    rounds(dve, seq, B, 1)

        layer_norm("ln1_", True)

        with ExitStack() as p:
            pq = [[ps(f"proj{j}{i}", on=p) for i in range(2)] for j in range(3)]
            vtp = [ps(f"vt_ps{i}", on=p) for i in range(2)]
            qs = [[sb(f"qkv{j}{i}", [C, T], on=p) for i in range(2)] for j in range(3)]
            parts = [[sb(f"parts{j}{i}", [C, PARTS, T], bf16, on=p) for i in range(2)] for j in range(2)]
            rest = [[sb(f"rest{j}{i}", [C, T], on=p) for i in range(2)] for j in range(2)]
            vt = [sb(f"vt{i}", [CH, NCH, HEADS, 2 * HD], on=p) for i in range(2)]
            one = sb("one", [C, 1], on=p)
            s_pr = [sem(f"proj_ready{j}") for j in range(3)]
            s_ge = [sem(f"gelu_ready{j}") for j in range(3)]
            s_split = [sem("q_split_steps"), sem("k_split_steps")]
            s_vt, s_vc, s_one = sem("v_transposed"), sem("v_copied"), sem("one_set")
            s_vone = sem("v_ones_set")
            s_store = [sem(f"qkv_stored{i}") for i in range(2)]
            block = p.enter_context(nc.Block())

            def stored(n):
                return 48 * (n // 2)

            @block.tensor
            def _(pe):
                def seq(n, par):
                    o = 1 - par
                    live = not (isinstance(n, int) and n >= B)
                    for j in (0, 1, None, 2):
                        if j is None:
                            if not (isinstance(n, int) and n == 0):
                                pe.wait_ge(s_ge[2], n)
                                at_least(pe, s_vc, n - 2)
                                for c in range(NCH):
                                    last = nc.tensor.transpose(vtp[o][0:CH, c * C:(c + 1) * C], qs[2][o][:, c * CH:(c + 1) * CH], ident)
                                last.then_inc(s_vt, 1)
                        elif live:
                            at_least(pe, s_ge[j], n - 1)
                            nc.tensor.matmul(pq[j][par][:, 0:T], aw[:, j, :], XH[:, n, :], start=True, stop=True).then_inc(s_pr[j], 1)

                rounds(pe, seq, B, 1)

            @block.scalar
            def _(act):
                nc.scalar.preload_act_table(ACT.Gelu)

                def seq(n, par):
                    for j in range(3):
                        act.wait_ge(s_pr[j], n + 1)
                        if j < 2:
                            at_least(act, s_split[j], 4 * (n - 1))
                        else:
                            at_least(act, s_vt, n - 1)
                        nc.scalar.activation(qs[j][par][:, :], pq[j][par][:, 0:T], ACT.Gelu, bias=ab[:, j:j + 1]).then_inc(s_ge[j], 1)

                rounds(act, seq, B)

            @block.vector
            def _(dve):
                def seq(n, par):
                    q, pa, r = qs[0][par], parts[0][par], rest[0][par]
                    dve.wait_ge(s_ge[0], n + 1)
                    if not (isinstance(n, int) and n < 2):
                        dve.wait_ge(s_store[par], stored(n))
                    nc.vector.tensor_scalar(pa[:, 0, :], q[:, :], 0.25, None, ALU.mult).then_inc(s_split[0], 1)
                    dve.wait_ge(s_split[0], 4 * n + 1)
                    nc.vector.scalar_tensor_tensor(r[:, :], q[:, :], 0.25, pa[:, 0, :], ALU.mult, ALU.subtract).then_inc(s_split[0], 1)
                    if not (isinstance(n, int) and n == 0):
                        copy_v(n - 1, 1 - par)
                    dve.wait_ge(s_split[0], 4 * n + 2)
                    nc.vector.tensor_copy(pa[:, 1, :], r[:, :]).then_inc(s_split[0], 1)
                    dve.wait_ge(s_split[0], 4 * n + 3)
                    nc.vector.tensor_tensor(pa[:, 2, :], r[:, :], pa[:, 1, :], ALU.subtract).then_inc(s_split[0], 1)

                def copy_v(n, par):
                    dve.wait_ge(s_vt, n + 1)
                    if not (isinstance(n, int) and n < 2):
                        dve.wait_ge(s_store[par], stored(n))
                    nc.vector.tensor_copy(vt[par][:, :, :, 0:HD].rearrange("p c h d -> p (c h) d"),
                                          vtp[par][0:CH, :].rearrange("p (c d) -> p c d", d=HD)).then_inc(s_vc, 1)

                for i in range(2):
                    nc.vector.memset(vt[i][:, :, :, HD:2 * HD], 1.0).then_inc(s_vone, 1)
                rounds(dve, seq, B)
                copy_v(B - 1, 1)

            @block.gpsimd
            def _(pool):
                nc.gpsimd.memset(one[:, :], 1.0).then_inc(s_one, 1)
                pool.wait_ge(s_one, 1)

                def seq(n, par):
                    k, pa, r = qs[1][par], parts[1][par], rest[1][par]
                    ones = one[:, 0:1].broadcast_to([C, T])
                    pool.wait_ge(s_ge[1], n + 1)
                    if not (isinstance(n, int) and n < 2):
                        pool.wait_ge(s_store[par], stored(n))
                    nc.gpsimd.tensor_tensor(pa[:, 0, :], k[:, :], ones, ALU.mult).then_inc(s_split[1], 1)
                    pool.wait_ge(s_split[1], 4 * n + 1)
                    nc.gpsimd.tensor_tensor(r[:, :], k[:, :], pa[:, 0, :], ALU.subtract).then_inc(s_split[1], 1)
                    pool.wait_ge(s_split[1], 4 * n + 2)
                    nc.gpsimd.tensor_tensor(pa[:, 1, :], r[:, :], ones, ALU.mult).then_inc(s_split[1], 1)
                    pool.wait_ge(s_split[1], 4 * n + 3)
                    nc.gpsimd.tensor_tensor(pa[:, 2, :], r[:, :], pa[:, 1, :], ALU.subtract).then_inc(s_split[1], 1)

                rounds(pool, seq, B)

            @block.sync
            def _(sp):
                def seq(n, par):
                    sp.wait_ge(s_par, 80)
                    sp.wait_ge(s_split[0], 4 * n + 4)
                    sp.dma_start(q_d[n], parts[0][par][:, :, :]).then_inc(s_store[par], 16)
                    sp.wait_ge(s_par, 80)
                    sp.wait_ge(s_split[1], 4 * n + 4)
                    sp.dma_start(k_d[n], parts[1][par][:, :, :]).then_inc(s_store[par], 16)
                    sp.wait_ge(s_par, 80)
                    sp.wait_ge(s_vone, 2)
                    sp.wait_ge(s_vc, n + 1)
                    sp.dma_start(v_d[n], vt[par][:, :, :, :]).then_inc(s_store[par], 16)

                rounds(sp, seq, B)
                sp.wait_ge(s_store[0], 24 * B)
                sp.wait_ge(s_store[1], 24 * B)

        with ExitStack() as p:
            HALF, HALVES = HEADS // 2, 2 * NCH
            ROWS = KROWS + PARTS
            qk = [sb(f"q_stack{i}", [ROWS, HEADS, T], bf16, on=p) for i in range(2)]
            kk = [sb(f"k_stack{i}", [ROWS, HEADS, T], bf16, on=p) for i in range(2)]
            vx = [sb(f"vx{i}", [CH, NCH, HEADS, 2 * HD], on=p) for i in range(2)]
            pt = [[sb(f"pt{i}{k}", [CH, HALF * CH], on=p) for k in range(NCH)] for i in range(2)]
            nm = [sb(f"nm{i}", [CH, HALF], on=p) for i in range(2)]
            nr = sb("nr", [CH, HALF], on=p)
            mp = [sb(f"mp{i}", [CH, PARTS, HALF], bf16, on=p) for i in range(2)]
            one = sb("one_a", [CH, 1], on=p)
            idb = sb("idb", [CH, CH], bf16, on=p)
            os = sb("os", [C, 2 * CH], on=p)
            ri = sb("ri", [CH, HEADS], on=p)
            of = sb("of", [CH, C], on=p)
            s_bank = [ps(f"s{i}", on=p) for i in range(2)]
            t_bank = [ps(f"t{i}", on=p) for i in range(2)]
            o_bank = [ps(f"o{i}", on=p) for i in range(2)]
            m_bank, f_bank = ps("m", on=p), ps("f", on=p)
            s_c = sem("constants_set")
            s_ld = [sem(f"qkv_loaded{i}") for i in range(2)]
            s_s, s_max, s_sp, s_row, s_rowc = (sem(n) for n in ("scores_ready", "max_ready", "max_split", "max_rows", "max_rows_copied"))
            s_st, s_exp, s_av = sem("scores_t_ready"), sem("exp_ready"), sem("av_done")
            s_oe, s_ta, s_ri, s_of, s_tb, s_fc = (sem(n) for n in ("o_in_sbuf", "o_turned", "sum_inverted", "o_scaled", "o_turned_back", "o_stored"))
            block = p.enter_context(nc.Block())
            LOADED = 16 * (2 * len(PAIRS) + 1)
            LAG = 2

            def batches(eng, seq):
                seq(0, 0)
                seq(1, 1)
                with eng.Fori(1, B // 2 - 1) as i:
                    seq(2 * i, 0)
                    seq(2 * i + 1, 1)
                seq(B - 2, 0)
                seq(B - 1, 1)

            def before(n, back):
                return isinstance(n, int) and n == 0 and back

            def final(n):
                return isinstance(n, int) and n == B - 1

            @block.sync
            def _(sp):
                def seq(n, par):
                    if not (isinstance(n, int) and n < 2):
                        sp.wait_ge(s_par, 80)
                        sp.wait_ge(s_av, (n - 1) * HALVES * NCH)
                    for a, (qp, kp) in enumerate(PAIRS):
                        at = slice(a * HD, (a + 1) * HD)
                        sp.dma_start(qk[par][at, :, :], q_d[n, :, qp, :].rearrange("(h d) t -> d h t", d=HD)).then_inc(s_ld[par], 16)
                        sp.dma_start(kk[par][at, :, :], k_d[n, :, kp, :].rearrange("(h d) t -> d h t", d=HD)).then_inc(s_ld[par], 16)
                    sp.dma_start(vx[par][:, :, :, :], v_d[n]).then_inc(s_ld[par], 16)

                rounds(sp, seq, B)

            @block.gpsimd
            def _(pool):
                nc.gpsimd.memset(one[:, :], 1.0).then_inc(s_c, 1)
                for i in range(2):
                    pool.wait_ge(s_c, i + 1)
                    nc.gpsimd.memset(kk[i][KROWS:ROWS, :, :], 1.0).then_inc(s_c, 1)
                pool.wait_ge(s_c, 3)
                nc.gpsimd.tensor_copy(idb[:, :], ident[0:CH, 0:CH]).then_inc(s_c, 1)
                pool.wait_ge(s_c, 4)

                def split(n, h, m):
                    g = n * HALVES + h
                    ones = one[:, 0:1].broadcast_to([CH, HALF])
                    pool.wait_ge(s_max, 4 * g + 4)
                    at_least(pool, s_row, g - 1)
                    nc.gpsimd.tensor_tensor(mp[m][:, 0, :], nm[m][:, :], ones, ALU.mult).then_inc(s_sp, 1)
                    pool.wait_ge(s_sp, 4 * g + 1)
                    nc.gpsimd.tensor_tensor(nr[:, :], nm[m][:, :], mp[m][:, 0, :], ALU.subtract).then_inc(s_sp, 1)
                    pool.wait_ge(s_sp, 4 * g + 2)
                    nc.gpsimd.tensor_tensor(mp[m][:, 1, :], nr[:, :], ones, ALU.mult).then_inc(s_sp, 1)
                    pool.wait_ge(s_sp, 4 * g + 3)
                    nc.gpsimd.tensor_tensor(mp[m][:, 2, :], nr[:, :], mp[m][:, 1, :], ALU.subtract).then_inc(s_sp, 1)

                def seq(n, par):
                    for h in range(HALVES):
                        split(n, h, h % 2)

                rounds(pool, seq, B)

            @block.tensor
            def _(pe):
                def scores(n, h, k, par):
                    c, j = h // 2, h % 2
                    if h == 0 and k == 0:
                        pe.wait_ge(s_ld[par], LOADED * (n // 2 + 1))
                    at_least(pe, s_max, 4 * (n * HALVES + h) + k - 1)
                    nc.tensor.matmul(s_bank[k % 2][0:CH, 0:T], qk[par][0:KROWS, HALF * j + k, c * CH:(c + 1) * CH],
                                     kk[par][0:KROWS, HALF * j + k, :], start=True, stop=True).then_inc(s_s, 1)

                def max_rows(n, h):
                    g = n * HALVES + h
                    pe.wait_ge(s_sp, 4 * g + 4)
                    at_least(pe, s_rowc, g)
                    for k in range(HALF):
                        last = nc.tensor.matmul(m_bank[KROWS:ROWS, k * CH:(k + 1) * CH], mp[h % 2][:, :, k], idb[:, :], start=True, stop=True)
                    last.then_inc(s_row, 1)

                def scores_t(n, h, k, par):
                    c, j, g = h // 2, h % 2, n * HALVES + h
                    if k == 0:
                        pe.wait_ge(s_rowc, g + 1)
                    at_least(pe, s_exp, 4 * g + k - 1)
                    for q in range(HALF):
                        last = nc.tensor.matmul(t_bank[k % 2][0:CH, q * CH:(q + 1) * CH], kk[par][:, HALF * j + q, k * CH:(k + 1) * CH],
                                                qk[par][:, HALF * j + q, c * CH:(c + 1) * CH], start=True, stop=True)
                    last.then_inc(s_st, 1)

                def times_v(n, h, k, par):
                    c, j, g = h // 2, h % 2, n * HALVES + h
                    pe.wait_ge(s_exp, 4 * g + k + 1)
                    if j == 0 and k == 0:
                        at_least(pe, s_oe, n * NCH + c - 1)
                    for q in range(HALF):
                        last = nc.tensor.matmul(o_bank[c % 2][32 * q:32 * q + 32, j * CH:(j + 1) * CH], vx[par][:, k, HALF * j + q, :],
                                                pt[h % 2][k][:, q * CH:(q + 1) * CH], start=k == 0, stop=k == NCH - 1)
                    last.then_inc(s_av, 1)

                def turn(u):
                    pe.wait_ge(s_oe, u + 1)
                    at_least(pe, s_fc, u)
                    for j in range(2):
                        last = nc.tensor.transpose(f_bank[0:CH, j * C:(j + 1) * C], os[:, j * CH:(j + 1) * CH], ident)
                    last.then_inc(s_ta, 1)

                def turn_back(u):
                    pe.wait_ge(s_of, u + 1)
                    nc.tensor.transpose(f_bank[:, 2 * C:2 * C + CH], of[:, :], ident[0:CH, 0:CH]).then_inc(s_tb, 1)

                def seq(n, par):
                    for h in range(HALVES):
                        c, j = h // 2, h % 2
                        u = n * NCH + c
                        for k in range(NCH):
                            if h + 2 < HALVES:
                                scores(n, h + 2, k, par)
                            elif not final(n):
                                scores(n + 1, h + 2 - HALVES, k, 1 - par)
                            scores_t(n, h, k, par)
                            if k >= LAG:
                                times_v(n, h, k - LAG, par)
                            elif h > 0:
                                times_v(n, h - 1, k - LAG + NCH, par)
                            elif not before(n, 1):
                                times_v(n - 1, HALVES - 1, k - LAG + NCH, 1 - par)
                            if k == 2:
                                if h + 1 < HALVES:
                                    max_rows(n, h + 1)
                                elif not final(n):
                                    max_rows(n + 1, 0)
                            if j == 1 and k == 1 and not before(n, c == 0):
                                turn(u - 1)
                            if j == 0 and k == 0 and not before(n, c < 2):
                                turn_back(u - 2)

                pe.wait_ge(s_c, 4)
                for h in range(2):
                    for k in range(NCH):
                        scores(0, h, k, 0)
                max_rows(0, 0)
                batches(pe, seq)
                for k in range(NCH - LAG, NCH):
                    times_v(B - 1, HALVES - 1, k, 1)
                turn_back(B * NCH - 2)
                turn(B * NCH - 1)
                turn_back(B * NCH - 1)

            @block.scalar
            def _(act):
                nc.scalar.preload_act_table(ACT.Exp)

                def copy_rows(n, h, par):
                    c, j, g = h // 2, h % 2, n * HALVES + h
                    act.wait_ge(s_row, g + 1)
                    nc.scalar.activation(qk[par][KROWS:ROWS, HALF * j:HALF * (j + 1), c * CH:(c + 1) * CH],
                                         m_bank[KROWS:ROWS, 0:HALF * CH].rearrange("p (h t) -> p h t", h=HALF), ACT.Copy).then_inc(s_rowc, 1)

                def take_o(u, par2):
                    act.wait_ge(s_av, 8 * u + 8)
                    at_least(act, s_ta, u)
                    nc.scalar.activation(os[:, :], o_bank[par2][:, 0:2 * CH], ACT.Copy).then_inc(s_oe, 1)

                def store_o(n, c):
                    act.wait_ge(s_tb, n * NCH + c + 1)
                    nc.scalar.activation(XH[:, n, c * CH:(c + 1) * CH], f_bank[:, 2 * C:2 * C + CH], ACT.Copy).then_inc(s_fc, 1)

                def seq(n, par):
                    for h in range(HALVES):
                        c, j, g = h // 2, h % 2, n * HALVES + h
                        u = n * NCH + c
                        for k in range(NCH):
                            act.wait_ge(s_st, 4 * g + k + 1)
                            at_least(act, s_av, 4 * g + k - 7)
                            nc.scalar.activation(pt[h % 2][k][:, :], t_bank[k % 2][0:CH, 0:HALF * CH], ACT.Exp).then_inc(s_exp, 1)
                            if k == 2:
                                if h + 1 < HALVES:
                                    copy_rows(n, h + 1, par)
                                elif not final(n):
                                    copy_rows(n + 1, 0, 1 - par)
                            if j == 0 and k == 3 and not before(n, c == 0):
                                take_o(u - 1, (c + 1) % 2)
                            if j == 0 and k == 1 and not before(n, c < 2):
                                store_o(n if c >= 2 else n - 1, (c - 2) % NCH)

                copy_rows(0, 0, 0)
                batches(act, seq)
                store_o(B - 1, NCH - 2)
                take_o(B * NCH - 1, 1)
                store_o(B - 1, NCH - 1)

            @block.vector
            def _(dve):
                def row_max(n, h, k):
                    g = n * HALVES + h
                    dve.wait_ge(s_s, 4 * g + k + 1)
                    if k == 0:
                        at_least(dve, s_sp, 4 * (g - 1))
                    nc.vector.tensor_reduce(nm[h % 2][:, k:k + 1], s_bank[k % 2][0:CH, 0:T], AX, ALU.max, negate=True).then_inc(s_max, 1)

                def scale_o(u):
                    dve.wait_ge(s_ta, u + 1)
                    at_least(dve, s_of, u)
                    turned = f_bank[0:CH, 0:2 * C].rearrange("p (h d) -> p h d", d=2 * HD)
                    nc.vector.reciprocal(ri[:, :].rearrange("p (h o) -> p h o", o=1), turned[:, :, HD:HD + 1]).then_inc(s_ri, 1)
                    dve.wait_ge(s_ri, u + 1)
                    at_least(dve, s_tb, u)
                    nc.vector.tensor_tensor(of[:, :].rearrange("p (h d) -> p h d", d=HD), turned[:, :, 0:HD],
                                            ri[:, :].rearrange("p (h o) -> p h o", o=1).broadcast_to([CH, HEADS, HD]), ALU.mult).then_inc(s_of, 1)

                def seq(n, par):
                    for h in range(HALVES):
                        c, j = h // 2, h % 2
                        for k in range(NCH):
                            if h + 2 < HALVES:
                                row_max(n, h + 2, k)
                            elif not final(n):
                                row_max(n + 1, h + 2 - HALVES, k)
                            if j == 1 and k == 2 and not before(n, c == 0):
                                scale_o(n * NCH + c - 1)

                for h in range(2):
                    for k in range(NCH):
                        row_max(0, h, k)
                batches(dve, seq)
                scale_o(B * NCH - 1)

        with ExitStack() as p:
            wps = [ps(f"wo_ps{i}", on=p) for i in range(2)]
            gb = [sb(f"gb{i}", [C, T], on=p) for i in range(2)]
            s_wo, s_go, s_add = sem("wo_ready"), sem("wo_gelu"), sem("residual_added")
            block = p.enter_context(nc.Block())

            @block.tensor
            def _(pe):
                def seq(n, par):
                    at_least(pe, s_go, n - 1)
                    nc.tensor.matmul(wps[par][:, 0:T], aw[:, 3, :], XH[:, n, :], start=True, stop=True).then_inc(s_wo, 1)

                rounds(pe, seq, B)

            @block.scalar
            def _(act):
                nc.scalar.preload_act_table(ACT.Gelu)

                def seq(n, par):
                    act.wait_ge(s_wo, n + 1)
                    at_least(act, s_add, n - 1)
                    nc.scalar.activation(gb[par][:, :], wps[par][:, 0:T], ACT.Gelu, bias=ab[:, 3:4]).then_inc(s_go, 1)

                rounds(act, seq, B)

            @block.vector
            def _(dve):
                def seq(n, par):
                    dve.wait_ge(s_go, n + 1)
                    nc.vector.tensor_tensor(Y[:, n, :], Y[:, n, :], gb[par][:, :], ALU.add).then_inc(s_add, 1)

                rounds(dve, seq, B)

        layer_norm("ln2_", False)

        with ExitStack() as p:
            FI, L, FIL = slice(0, 2 * C), slice(2 * C, 2 * C + S), slice(0, 2 * C + S)
            G, O = slice(2 * C + S, 3 * C + S), slice(3 * C + S, 4 * C + S)
            W_ALL = 4 * C + S
            wx, wh = sb("wx", [C, S, W_ALL], on=p), sb("wh", [C, S, W_ALL], on=p)
            wc = sb("wc", [C, S], on=p)
            rows = 3 * S
            bi, bh = sb("bi", [rows, W_ALL], on=p), sb("bh", [rows, W_ALL], on=p)
            bsplit = [sb(f"bsplit{i}", [rows, W_ALL], bf16, on=p) for i in range(3)]
            bw = sb("bw", [rows, W_ALL], bf16, on=p)
            ind = sb("ind", [rows, C], bf16, on=p)
            xs = sb("xs", [C, STEPS, B], on=p)
            hs = sb("hs", [C, STEPS, B], on=p)
            cs = [sb(f"cs{i}", [C, B], on=p) for i in range(2)]
            ob = [sb(f"ob{i}", [C, 4, B], on=p) for i in range(4)]
            fi = [sb(f"fi{i}", [C, 2 * C], on=p) for i in range(2)]
            tg = [sb(f"tg{i}", [C, C], on=p) for i in range(2)]
            to = [sb(f"to{i}", [C, C], on=p) for i in range(2)]
            tc = [sb(f"tc{i}", [C, B], on=p) for i in range(2)]
            uu, vv = sb("uu", [C, C], on=p), sb("vv", [C, C], on=p)
            c2 = sb("c2", [C, C], on=p)
            lg = [sb(f"lg{i}", [C, S], on=p) for i in range(2)]
            lm, lq, le = sb("lm", [C, 1], on=p), sb("lq", [C, 1], on=p), sb("le", [C, S], on=p)
            sel = sb("sel", [C, C], on=p)
            zero = sb("zero", [C, B], on=p)
            g_fi, g_g, g_o = ps("g_fi", on=p), ps("g_g", on=p), ps("g_o", on=p)
            hc, ot = ps("hc", on=p), ps("ot", on=p)
            cr = ps("cr", on=p)
            s_w, s_sc, s_bz = sem("lstm_loaded"), sem("lstm_scaled"), sem("bias_chain")
            s_z = sem("state_zeroed")
            s_xs, s_xu = sem("x_staged"), sem("x_used")
            s_fi, s_lg, s_g, s_o = sem("fi_logits_ready"), sem("logits_in_sbuf"), sem("g_ready"), sem("o_ready")
            s_tfi, s_tg, s_to, s_tc, s_cc = sem("fi_tanh"), sem("g_tanh"), sem("o_tanh"), sem("c_tanh"), sem("c_copied")
            s_m, s_q, s_sel = sem("logit_max"), sem("chosen"), sem("sel_ready")
            s_u, s_v, s_c2, s_h = sem("u_ready"), sem("v_ready"), sem("c2_ready"), sem("h_ready")
            s_crep, s_hc, s_ot = sem("crep_ready"), sem("chosen_c_ready"), sem("chosen_o_ready")
            s_ob, s_out = sem("out_ready"), [sem(f"out_stored{i}") for i in range(4)]
            block = p.enter_context(nc.Block())
            NB = T // STEPS
            QS = STEPS // 4
            LOADS = 3 + 2 * 3

            @block.sync
            def _(sp):
                sp.dma_start(wx[:, :, :], w_ih).then_inc(s_w, 16)
                sp.dma_start(wh[:, :, :], w_hh).then_inc(s_w, 16)
                sp.dma_start(wc[:, :], w_selc).then_inc(s_w, 16)
                for k in range(3):
                    sp.dma_start(bi[k * S:(k + 1) * S, :], b_ih).then_inc(s_w, 16)
                    sp.dma_start(bh[k * S:(k + 1) * S, :], b_hh).then_inc(s_w, 16)

                def body(it):
                    for q in range(QS):
                        sp.wait_ge(s_par, 80)
                        sp.wait_ge(s_ob, it * QS + q + 1)
                        sp.dma_start(out[:, bass.ds(it * STEPS + 4 * q, 4), :], ob[q][:, :, :]).then_inc(s_out[q], 16)

                body(0)
                with sp.Fori(1, NB) as it:
                    body(it)
                for q in range(QS):
                    sp.wait_ge(s_out[q], 16 * NB)

            @block.gpsimd
            def _(pool):
                def stage(it, q, first):
                    pool.wait_ge(s_par, 80)
                    if not first:
                        pool.wait_ge(s_xu, (it - 1) * STEPS + 4 * q + 4)
                    nc.gpsimd.tensor_copy(xs[:, 4 * q:4 * q + 4, :],
                                          XH[:, :, bass.ds(it * STEPS + 4 * q, 4)].rearrange("p b t -> p t b")).then_inc(s_xs, 1)

                def body(it, first, last):
                    for q in range(QS):
                        if not last:
                            stage(it + 1, q, False)
                        pool.wait_ge(s_h, it * STEPS + 4 * q + 4)
                        if not first:
                            pool.wait_ge(s_out[q], it * 16)
                        nc.gpsimd.tensor_tensor(ob[q][:, :, :], hs[:, 4 * q:4 * q + 4, :],
                                                Y[:, :, bass.ds(it * STEPS + 4 * q, 4)].rearrange("p b t -> p t b"),
                                                ALU.add).then_inc(s_ob, 1)

                for q in range(QS):
                    stage(0, q, True)
                body(0, True, False)
                with pool.Fori(1, NB - 1) as it:
                    body(it, False, False)
                body(NB - 1, False, True)

            @block.tensor
            def _(pe):
                def x_part(bank, cols, k):
                    n = cols.stop - cols.start
                    for s in range(S):
                        nc.tensor.matmul(bank[32 * s:32 * s + 32, 0:n], xs[:, k, :], wx[:, s, cols],
                                         start=True, stop=False, skip_group_check=True)
                    return nc.tensor.matmul(bank[:, 0:n], ind[:, :], bw[:, cols], start=False, stop=False, skip_group_check=True)

                def state_part(bank, state, w, cols, stop=True):
                    n = cols.stop - cols.start
                    for s in range(S):
                        last = nc.tensor.matmul(bank[32 * s:32 * s + 32, 0:n], state, w[:, s, cols] if w is wh else w,
                                                start=False, stop=stop, skip_group_check=True)
                    return last

                def step(it, k, first, last):
                    t = it * STEPS + k
                    if not first:
                        pe.wait_ge(s_cc, t)
                    state_part(g_fi[:, L], zero[:, :] if first else cs[(k - 1) % 2][:, :], wc[:, :], L, False)
                    hk = zero[:, :] if first else hs[:, (k - 1) % STEPS, :]
                    if not first:
                        pe.wait_ge(s_h, t)
                    state_part(g_fi, hk, wh, FIL).then_inc(s_fi, 1)
                    state_part(g_g, hk, wh, G).then_inc(s_g, 1)
                    state_part(g_o, hk, wh, O).then_inc(s_o, 1)
                    nk = (k + 1) % STEPS
                    if not last:
                        if nk % 4 == 0:
                            pe.wait_ge(s_xs, it * QS + (k + 1) // 4 + 1)
                        pe.wait_ge(s_tfi, t + 1)
                        x_part(g_fi, FIL, nk)
                        pe.wait_ge(s_tg, t + 1)
                        x_part(g_g, G, nk)
                    pe.wait_ge(s_sel, t + 1)
                    pe.wait_ge(s_v, t + 1)
                    nc.tensor.matmul(hc[:, 0:B], vv[:, :], sel[:, 0:B], start=True, stop=False, skip_group_check=True)
                    pe.wait_ge(s_u, t + 1)
                    nc.tensor.matmul(hc[:, 0:B], uu[:, :], sel[:, 0:B], start=False, stop=True, skip_group_check=True).then_inc(s_hc, 1)
                    pe.wait_ge(s_to, t + 1)
                    nc.tensor.matmul(ot[:, 0:B], to[k % 2][:, :], sel[:, 0:B], start=True, stop=True).then_inc(s_ot, 1)
                    if not last:
                        x_part(g_o, O, nk).then_inc(s_xu, 1)
                        pe.wait_ge(s_c2, t + 1)
                        nc.tensor.matmul(cr[:, 0:C], sel[:, :], c2[:, :], start=True, stop=True).then_inc(s_crep, 1)

                def body(it, first, last):
                    for k in range(STEPS):
                        step(it, k, first and k == 0, last and k == STEPS - 1)

                pe.wait_ge(s_w, 16 * LOADS)
                pe.wait_ge(s_sc, 4)
                pe.wait_ge(s_z, 1)
                pe.wait_ge(s_xs, 1)
                x_part(g_fi, FIL, 0)
                x_part(g_g, G, 0)
                x_part(g_o, O, 0).then_inc(s_xu, 1)
                body(0, True, False)
                with pe.Fori(1, NB - 1) as it:
                    body(it, False, False)
                body(NB - 1, False, True)

            @block.scalar
            def _(act):
                nc.scalar.preload_act_table(ACT.Tanh)

                def step(t, k):
                    par = k % 2
                    act.wait_ge(s_fi, t + 1)
                    nc.scalar.activation(lg[par][:, :], g_fi[:, L], ACT.Copy).then_inc(s_lg, 1)
                    nc.scalar.activation(fi[par][:, :], g_fi[:, 0:2 * C], ACT.Tanh).then_inc(s_tfi, 1)
                    act.wait_ge(s_g, t + 1)
                    nc.scalar.activation(tg[par][:, :], g_g[:, 0:C], ACT.Tanh).then_inc(s_tg, 1)
                    act.wait_ge(s_o, t + 1)
                    nc.scalar.activation(to[par][:, :], g_o[:, 0:C], ACT.Tanh).then_inc(s_to, 1)
                    act.wait_ge(s_hc, t + 1)
                    nc.scalar.activation(tc[par][:, :], hc[:, 0:B], ACT.Tanh).then_inc(s_tc, 1)
                    nc.scalar.activation(cs[par][:, :], hc[:, 0:B], ACT.Copy).then_inc(s_cc, 1)

                def body(it):
                    for k in range(STEPS):
                        step(it * STEPS + k, k)

                body(0)
                with act.Fori(1, NB) as it:
                    body(it)

            @block.vector
            def _(dve):
                nc.vector.memset(zero[:, :], 0.0).then_inc(s_z, 1)
                dve.wait_ge(s_w, 16 * LOADS)
                OG = slice(3 * C + S, 4 * C + S)
                for w in (wx, wh):
                    nc.vector.tensor_scalar(w[:, :, FI], w[:, :, FI], 0.5, None, ALU.mult).then_inc(s_bz, 1)
                    nc.vector.tensor_scalar(w[:, :, OG], w[:, :, OG], 0.5, None, ALU.mult).then_inc(s_bz, 1)
                nc.vector.tensor_copy(ind[:, :], kc[0:rows, COLS[K_IND]:COLS[K_IND] + C]).then_inc(s_bz, 1)
                nc.vector.tensor_tensor(bi[:, :], bi[:, :], bh[:, :], ALU.add).then_inc(s_bz, 1)
                dve.wait_ge(s_bz, 6)
                nc.vector.tensor_scalar(bi[:, FI], bi[:, FI], 0.5, None, ALU.mult).then_inc(s_bz, 1)
                nc.vector.tensor_scalar(bi[:, OG], bi[:, OG], 0.5, None, ALU.mult).then_inc(s_bz, 1)
                dve.wait_ge(s_bz, 8)
                nc.vector.tensor_copy(bsplit[0][:, :], bi[:, :]).then_inc(s_bz, 1)
                dve.wait_ge(s_bz, 9)
                nc.vector.tensor_tensor(bi[:, :], bi[:, :], bsplit[0][:, :], ALU.subtract).then_inc(s_bz, 1)
                dve.wait_ge(s_bz, 10)
                nc.vector.tensor_copy(bsplit[1][:, :], bi[:, :]).then_inc(s_bz, 1)
                dve.wait_ge(s_bz, 11)
                nc.vector.tensor_tensor(bi[:, :], bi[:, :], bsplit[1][:, :], ALU.subtract).then_inc(s_bz, 1)
                dve.wait_ge(s_bz, 12)
                nc.vector.tensor_copy(bsplit[2][:, :], bi[:, :]).then_inc(s_bz, 1)
                part = kc[0:rows, COLS[K_PART]:COLS[K_PART] + 3]
                nc.vector.tensor_scalar(bw[:, :], bsplit[0][:, :], part[:, 0:1], None, ALU.mult).then_inc(s_bz, 1)
                dve.wait_ge(s_bz, 14)
                for k in (1, 2):
                    nc.vector.scalar_tensor_tensor(bw[:, :], bsplit[k][:, :], part[:, k:k + 1], bw[:, :], ALU.mult, ALU.add).then_inc(s_bz, 1)
                    dve.wait_ge(s_bz, 14 + k)
                nc.vector.engine_nop().then_inc(s_sc, 4)

                def step(it, k, first, early):
                    t = it * STEPS + k
                    par = k % 2
                    if first:
                        nc.vector.tensor_copy(sel[:, :], const(K_SEL0)).then_inc(s_sel, 1)
                    else:
                        dve.wait_ge(s_lg, t + 1)
                        nc.vector.tensor_reduce(lm[:, :], lg[par][:, :], AX, ALU.max).then_inc(s_m, 1)
                        dve.wait_ge(s_m, t)
                        nc.vector.scalar_tensor_tensor(le[:, :], lg[par][:, :], lm[:, 0:1], first_w, ALU.is_ge, ALU.mult,
                                                       accum_out=lq[:, :]).then_inc(s_q, 1)
                    dve.wait_ge(s_tfi, t + 1)
                    if first:
                        nc.vector.memset(vv[:, :], 0.0).then_inc(s_v, 1)
                    else:
                        dve.wait_ge(s_crep, t)
                        nc.vector.scalar_tensor_tensor(vv[:, :], fi[par][:, 0:C], 1.0, cr[:, 0:C], ALU.add, ALU.mult).then_inc(s_v, 1)
                    dve.wait_ge(s_tg, t + 1)
                    nc.vector.scalar_tensor_tensor(uu[:, :], fi[par][:, C:2 * C], 1.0, tg[par][:, :], ALU.add, ALU.mult).then_inc(s_u, 1)
                    if not first:
                        dve.wait_ge(s_q, t)
                        nc.vector.tensor_scalar(sel[:, :], pick, lq[:, 0:1], 0.0, ALU.mult, ALU.max).then_inc(s_sel, 1)
                    dve.wait_ge(s_v, t + 1)
                    dve.wait_ge(s_u, t + 1)
                    nc.vector.tensor_tensor(c2[:, :], uu[:, :], vv[:, :], ALU.add).then_inc(s_c2, 1)
                    dve.wait_ge(s_ot, t + 1)
                    if k % 4 == 0 and not early:
                        dve.wait_ge(s_ob, it * QS + k // 4 - QS + 1)
                    dve.wait_ge(s_tc, t + 1)
                    nc.vector.scalar_tensor_tensor(hs[:, k, :], ot[:, 0:B], 0.5, tc[par][:, :], ALU.add, ALU.mult).then_inc(s_h, 1)

                def body(it, early):
                    for k in range(STEPS):
                        step(it, k, early and k == 0, early)

                body(0, True)
                with dve.Fori(1, NB) as it:
                    body(it, False)


def constants():
    import numpy as np
    k = np.zeros((128, COLS[-1]), np.float32)
    p = np.arange(128)

    def put(which, a):
        k[:a.shape[0], COLS[which]:COLS[which] + a.shape[1]] = a

    same = (p[:, None] % 32 == p[None, :] % 32).astype(np.float32)
    put(K_ID, np.eye(128, dtype=np.float32))
    put(K_PICK, 0.5 * same)
    put(K_CENTRE, np.eye(128, dtype=np.float32) - np.float32(1 / 128))
    put(K_MEAN, np.full((128, 128), 1 / 128, np.float32))
    module, s = p[:, None] // 32, np.arange(S)[None, :]
    put(K_FIRST, np.where(s == module, 1, np.where(s < module, -8, 0)).astype(np.float32))
    put(K_IND, (np.arange(3 * S)[:, None] % S == p[None, :] // 32).astype(np.float32))
    put(K_PART, (np.arange(3 * S)[:, None] // S == np.arange(3)[None, :]).astype(np.float32))
    put(K_SEL0, 0.5 * same * (p[:, None] < 32))
    return k


def kernel(**inputs):
    import numpy as np
    import concourse.bacc as bacc
    from concourse.bass_utils import run_bass_kernel_spmd

    a = {k: np.asarray(v) for k, v in inputs.items()}
    gates = [1, 0, 2, 3]

    def lstm_w(w, w_sel):
        g = w.reshape(S, 4, C, C)[:, gates].reshape(S, 4 * C, C)
        sel = np.broadcast_to(w_sel, (S, S, C))
        return np.concatenate([g[:, :2 * C], sel, g[:, 2 * C:]], 1).transpose(2, 0, 1)

    def lstm_b(b, b_sel):
        g = b.reshape(S, 4, C)[:, gates].reshape(S, 4 * C)
        return np.concatenate([g[:, :2 * C], np.broadcast_to(b_sel, (S, S)), g[:, 2 * C:]], 1)

    tok = a["L0_tok_W"].T
    tokw = np.zeros((128, 3, C), np.float32)
    tokw[:, 0], tokw[:, 1], tokw[:D, 2] = tok[0:128], tok[128:256], tok[256:320]
    w_sel = a["L0_ffn_W_sel"].reshape(S, 3, C)
    consts = constants()
    data = {
        "x": a["x"].transpose(2, 0, 1).reshape(D, B * T_IN),
        "tok_w": tokw,
        "tok_v": np.stack([a["L0_tok_b"], a["L0_tok_gamma"], a["L0_tok_beta"]], 1),
        "attn_w": np.stack([a[f"L0_attn_W{n}"].T for n in "qkvo"], 1),
        "attn_b": np.stack([a[f"L0_attn_b{n}"] for n in "qkvo"], 1),
        "w_ih": lstm_w(a["L0_ffn_W_ih"], w_sel[:, 2]),
        "w_hh": lstm_w(a["L0_ffn_W_hh"], w_sel[:, 0]),
        "w_selc": w_sel[:, 1].T,
        "b_ih": lstm_b(a["L0_ffn_b_ih"], a["L0_ffn_b_sel"]),
        "b_hh": lstm_b(a["L0_ffn_b_hh"], np.zeros(S, np.float32)),
        "consts": consts,
    }
    nc = bacc.Bacc("TRN2", target_bir_lowering=False, num_devices=1)
    arrays, args = {}, []
    for name, v in data.items():
        v = np.ascontiguousarray(v)
        arrays[name + "_dram"] = v
        args.append(nc.dram_tensor(name + "_dram", v.shape, mybir.dt.from_np(v.dtype), kind="ExternalInput").ap())
    out = nc.dram_tensor("out_dram", (C, T, B), mybir.dt.float32, kind="ExternalOutput").ap()
    audio_tower(nc, *args, out)
    r = run_bass_kernel_spmd(nc, [arrays], core_ids=[0])
    return np.ascontiguousarray(np.asarray(r.results[0]["out_dram"]).transpose(2, 1, 0))
```
